# Optimizing a Trainium2 kernel written in Bass

```python
import numpy as np
import jax
import jax.numpy as jnp

def _softmax(x, axis=-1):
    return jax.nn.softmax(x, axis=axis)

def _gelu(x):
    return jax.nn.gelu(x, approximate=True)

def _silu(x):
    return jax.nn.silu(x)

def _sigmoid(x):
    return jax.nn.sigmoid(x)

def _layernorm(x, axis=-1, eps=1e-05):
    m = jnp.mean(x, axis=axis, keepdims=True)
    v = jnp.var(x, axis=axis, keepdims=True)
    return (x - m) / jnp.sqrt(v + eps)

def _scatter_add(tgt, idx, src, axis=0):
    return tgt.at[idx].add(src)

def _segment_sum(src, seg, n):
    return jax.ops.segment_sum(src, seg, n)
kernel_name = 'mk_seq_postln_d4_jaxref_r8_a049ac'

def setup_inputs(seed: int=0):
    np.random.seed(seed)
    _w = jnp.asarray

    def _L0_attn_setup():
        import jax, jax.numpy as jnp
        import numpy as np
        EMBED_DIM = 128
        NUM_HEADS = 16
        HEAD_DIM = EMBED_DIM // NUM_HEADS
        SEQ_LEN = 128
        BATCH = 4
        MAX_REL_POS = 2

        def _rel_index(length_q, length_k):
            q = jnp.arange(length_q)[:, None]
            k = jnp.arange(length_k)[None, :]
            return jnp.clip(k - q, -MAX_REL_POS, MAX_REL_POS) + MAX_REL_POS
        key = jax.random.key(seed)
        ks = jax.random.split(key, 12)
        s = 1.0 / np.sqrt(EMBED_DIM)
        x = jax.random.normal(ks[0], (BATCH, SEQ_LEN, EMBED_DIM), dtype=jnp.float32)
        W_q = jax.random.normal(ks[1], (EMBED_DIM, EMBED_DIM), dtype=jnp.float32) * s
        b_q = jnp.zeros((EMBED_DIM,), dtype=jnp.float32)
        W_k = jax.random.normal(ks[2], (EMBED_DIM, EMBED_DIM), dtype=jnp.float32) * s
        b_k = jnp.zeros((EMBED_DIM,), dtype=jnp.float32)
        W_v = jax.random.normal(ks[3], (EMBED_DIM, EMBED_DIM), dtype=jnp.float32) * s
        b_v = jnp.zeros((EMBED_DIM,), dtype=jnp.float32)
        W_o = jax.random.normal(ks[4], (EMBED_DIM, EMBED_DIM), dtype=jnp.float32) * s
        b_o = jnp.zeros((EMBED_DIM,), dtype=jnp.float32)
        lim = float(np.sqrt(6.0 / (2 * MAX_REL_POS + 1 + HEAD_DIM)))
        rel_k_table = jax.random.uniform(ks[5], (2 * MAX_REL_POS + 1, HEAD_DIM), jnp.float32, -lim, lim)
        rel_v_table = jax.random.uniform(ks[6], (2 * MAX_REL_POS + 1, HEAD_DIM), jnp.float32, -lim, lim)
        return {'x': x, 'W_q': W_q, 'b_q': b_q, 'W_k': W_k, 'b_k': b_k, 'W_v': W_v, 'b_v': b_v, 'W_o': W_o, 'b_o': b_o, 'rel_k_table': rel_k_table, 'rel_v_table': rel_v_table}
    _L0_attn_in = _L0_attn_setup()

    def _L0_ffn_setup():
        import jax, jax.numpy as jnp
        import numpy as np
        B, S, D, F, E, K = (4, 256, 128, 512, 4, 2)
        key = jax.random.key(seed)
        k = jax.random.split(key, 6)
        x = jax.random.normal(k[0], (B, S, D), jnp.float32)
        router_w = jax.random.normal(k[1], (D, E), jnp.float32) * D ** (-0.5)
        router_b = jnp.zeros((E,), jnp.float32)
        w1 = jax.random.normal(k[2], (E, D, F), jnp.float32) * 0.02
        w3 = jax.random.normal(k[3], (E, D, F), jnp.float32) * 0.02
        w2 = jax.random.normal(k[4], (E, F, D), jnp.float32) * 0.02
        return {'x': x, 'router_w': router_w, 'router_b': router_b, 'w1': w1, 'w3': w3, 'w2': w2}
    _L0_ffn_in = _L0_ffn_setup()

    def _L1_attn_setup():
        import jax, jax.numpy as jnp
        import numpy as np
        H = 16
        WIN = 64
        key = jax.random.key(seed)
        ks = jax.random.split(key, 4)
        B, S, D = (1, 512, 128)
        s = 1.0 / np.sqrt(D)
        x = jax.random.normal(ks[0], (B, S, D), jnp.float32)
        Wqkv = jax.random.normal(ks[1], (3 * D, D), jnp.float32) * s
        bqkv = jnp.zeros((3 * D,), jnp.float32)
        Wout = jax.random.normal(ks[2], (D, D), jnp.float32) * s
        bout = jnp.zeros((D,), jnp.float32)
        return {'x': x, 'Wqkv': Wqkv, 'bqkv': bqkv, 'Wout': Wout, 'bout': bout}
    _L1_attn_in = _L1_attn_setup()

    def _L1_ffn_setup():
        import jax, jax.numpy as jnp
        import numpy as np
        TOP_K = 2
        key = jax.random.key(seed)
        k1, k2, k3, k4 = jax.random.split(key, 4)
        B, T, D, H, E = (2, 256, 128, 256, 8)
        x = jax.random.normal(k1, (B, T, D), dtype=jnp.float32)
        w12 = jax.random.normal(k2, (E, 2 * H, D), dtype=jnp.float32) * D ** (-0.5)
        w3 = jax.random.normal(k3, (E, D, H), dtype=jnp.float32) * H ** (-0.5)
        gate_w = jax.random.normal(k4, (E, D), dtype=jnp.float32) * D ** (-0.5)
        return {'x': x, 'w12': w12, 'w3': w3, 'gate_w': gate_w}
    _L1_ffn_in = _L1_ffn_setup()

    def _L2_attn_setup():
        import jax, jax.numpy as jnp
        import numpy as np
        import math
        HEADS = 16
        SEG = 32
        DIL = 4
        BLOCK_M = 64

        def _hilbert_points(level, x=0, y=0, xi=1, xj=0, yi=0, yj=1):
            if level <= 0:
                yield (x, y)
            else:
                for pt in _hilbert_points(level - 1, x, y, yi // 2, yj // 2, xi // 2, xj // 2):
                    yield pt
                for pt in _hilbert_points(level - 1, x + xi // 2, y + xj // 2, xi // 2, xj // 2, yi // 2, yj // 2):
                    yield pt
                for pt in _hilbert_points(level - 1, x + xi // 2 + yi // 2, y + xj // 2 + yj // 2, xi // 2, xj // 2, yi // 2, yj // 2):
                    yield pt
                for pt in _hilbert_points(level - 1, x + xi // 2 + yi, y + xj // 2 + yj, -yi // 2, -yj // 2, -xi // 2, -xj // 2):
                    yield pt

        def create_hilbert_mapping(seq_len):
            grid = 2 ** int(math.ceil(math.log2(math.sqrt(seq_len))))
            pts = list(_hilbert_points(int(math.log2(grid)), 0, 0, grid, 0, 0, grid))
            m = np.zeros(seq_len, dtype=np.int32)
            for hidx, (x, y) in enumerate(pts[:seq_len]):
                lin = y * grid + x
                if lin < seq_len:
                    m[lin] = hidx
            return jnp.asarray(m)

        def _hilbert_attention(x, Wqkv, bqkv, Wproj, bproj, mapping):
            B, M, dim = x.shape
            H = HEADS
            D = dim // H
            scale = D ** (-0.5)
            qkv = (x @ Wqkv + bqkv).reshape(B, M, 3, H, D)
            qkv = jnp.transpose(qkv, (2, 0, 3, 1, 4))
            q, k, v = (qkv[0], qkv[1], qkv[2])
            nb = M // BLOCK_M
            rm = jnp.arange(M).reshape(nb, BLOCK_M)
            mrm = mapping[rm].astype(jnp.int32)
            seg_idx = mrm // SEG
            offs = jnp.arange(0, SEG, DIL)
            key_pos = seg_idx[:, :, None] * SEG + offs[None, None, :]
            mask_k = key_pos < M
            kp0 = key_pos[:, 0, :]
            mask0 = mask_k[:, 0, :]
            idx0 = jnp.where(mask0, mapping[jnp.clip(kp0, 0, M - 1)], 0)
            Ksel = k[:, :, idx0, :] * mask0[None, None, :, :, None]
            Vsel = v[:, :, idx0, :] * mask0[None, None, :, :, None]
            qm = q[:, :, mrm, :] * scale
            scores = jnp.einsum('bhnmd,bhnsd->bhnms', qm, Ksel)
            scores = jnp.where(mask_k[None, None], scores, -1000000000.0)
            sexp = jnp.exp(scores - jnp.max(scores, axis=3, keepdims=True))
            acc = jnp.einsum('bhnms,bhnsd->bhnmd', sexp, Vsel)
            lsum = 1e-06 + jnp.sum(sexp, axis=-1)
            out = acc / lsum[..., None]
            out = out.reshape(B, H, M, D).transpose(0, 2, 1, 3).reshape(B, M, dim)
            return out @ Wproj + bproj
        key = jax.random.key(seed)
        ks = jax.random.split(key, 5)
        B, M, dim = (2, 512, 128)
        s = 1.0 / math.sqrt(dim)
        return {'x': jax.random.normal(ks[0], (B, M, dim), jnp.float32), 'Wqkv': jax.random.normal(ks[1], (dim, 3 * dim), jnp.float32) * s, 'bqkv': jax.random.normal(ks[2], (3 * dim,), jnp.float32) * 0.01, 'Wproj': jax.random.normal(ks[3], (dim, dim), jnp.float32) * s, 'bproj': jax.random.normal(ks[4], (dim,), jnp.float32) * 0.01, 'mapping': create_hilbert_mapping(M)}
    _L2_attn_in = _L2_attn_setup()

    def _L2_ffn_setup():
        import jax, jax.numpy as jnp
        import numpy as np
        D_MODEL = 128
        EXPANSION = 4
        D_HIDDEN = D_MODEL * EXPANSION
        NUM_STAGES = int(np.log2(D_HIDDEN))

        def butterfly(y, weights, dim):
            lead = y.shape[:-1]
            for stage in range(weights.shape[0]):
                s = 2 ** stage
                nb = dim // (2 * s)
                yr = y.reshape(*lead, nb, 2, s)
                a = yr[..., 0, :]
                b = yr[..., 1, :]
                w = weights[stage].reshape(nb, s, 2, 2)
                na = w[..., 0, 0] * a + w[..., 0, 1] * b
                nb2 = w[..., 1, 0] * a + w[..., 1, 1] * b
                y = jnp.stack([na, nb2], axis=-2).reshape(*lead, dim)
            return y
        key = jax.random.key(seed)
        ks = jax.random.split(key, 6)
        B, S = (4, 256)
        x = jax.random.normal(ks[0], (B, S, D_MODEL), jnp.float32)
        W_exp = jax.random.normal(ks[1], (D_MODEL, D_HIDDEN), jnp.float32) * 0.02
        b_exp = jnp.zeros((D_HIDDEN,), jnp.float32)
        up_weights = jax.random.normal(ks[2], (NUM_STAGES, D_HIDDEN // 2, 2, 2), jnp.float32) * 0.02
        up_bias = jnp.zeros((D_HIDDEN,), jnp.float32)
        down_weights = jax.random.normal(ks[3], (NUM_STAGES, D_HIDDEN // 2, 2, 2), jnp.float32) * 0.02
        W_con = jax.random.normal(ks[4], (D_HIDDEN, D_MODEL), jnp.float32) * 0.02
        b_con = jnp.zeros((D_MODEL,), jnp.float32)
        down_bias = jnp.zeros((D_MODEL,), jnp.float32)
        return dict(x=x, W_exp=W_exp, b_exp=b_exp, up_weights=up_weights, up_bias=up_bias, down_weights=down_weights, W_con=W_con, b_con=b_con, down_bias=down_bias)
    _L2_ffn_in = _L2_ffn_setup()

    def _L3_attn_setup():
        import jax, jax.numpy as jnp
        import numpy as np
        D_K, HEADS, K_BITS, L_TABLES = (128, 16, 4, 8)
        HEAD_DIM = D_K // HEADS
        R = 1 << K_BITS
        S = L_TABLES * R
        B, T = (4, 512)

        def _protos_T():
            r = np.arange(R)
            bits = r[:, None] >> K_BITS - 1 - np.arange(K_BITS) & 1
            corners = (2.0 * bits - 1.0).astype(np.float32)
            return jnp.asarray(corners.T)
        key = jax.random.key(seed)
        ks = jax.random.split(key, 7)
        x = jax.random.normal(ks[0], (B, T, D_K), dtype=jnp.float32)
        sc = 0.02
        Wq = jax.random.normal(ks[1], (D_K, D_K), dtype=jnp.float32) * sc
        Wk = jax.random.normal(ks[2], (D_K, D_K), dtype=jnp.float32) * sc
        Wv = jax.random.normal(ks[3], (D_K, D_K), dtype=jnp.float32) * sc
        Wo = jax.random.normal(ks[4], (D_K, D_K), dtype=jnp.float32) * sc
        bo = jnp.zeros((D_K,), dtype=jnp.float32)
        planes = jax.random.normal(ks[5], (L_TABLES * K_BITS, HEAD_DIM), dtype=jnp.float32)
        planes_T = planes.T
        logit_temp = jnp.zeros((), dtype=jnp.float32)
        protos_T = _protos_T()
        return {'x': x, 'Wq': Wq, 'Wk': Wk, 'Wv': Wv, 'Wo': Wo, 'bo': bo, 'planes_T': planes_T, 'protos_T': protos_T, 'logit_temp': logit_temp}
    _L3_attn_in = _L3_attn_setup()

    def _L3_ffn_setup():
        import jax, jax.numpy as jnp
        import numpy as np
        D_IN, D_HID = (128, 512)

        def _ternary(key, shape):
            return jax.random.randint(key, shape, -1, 2).astype(jnp.float32)

        def _tlin(x, w, s):
            return jnp.einsum('bsi,oi->bso', x, w) * s
        key = jax.random.key(seed)
        ks = jax.random.split(key, 12)
        inv = lambda fan: 1.0 / np.sqrt(fan).astype(np.float32)
        return {'x': jax.random.normal(ks[0], (4, 256, D_IN), dtype=jnp.float32), 'w1_w': _ternary(ks[1], (D_HID, D_IN)), 'w1_s': jax.random.uniform(ks[2], (D_HID,), dtype=jnp.float32) * inv(D_IN), 'w2_w': _ternary(ks[3], (D_HID, D_IN)), 'w2_s': jax.random.uniform(ks[4], (D_HID,), dtype=jnp.float32) * inv(D_IN), 'h1_w': _ternary(ks[5], (D_HID, D_HID)), 'h1_s': jax.random.uniform(ks[6], (D_HID,), dtype=jnp.float32) * inv(D_HID), 'h2_w': _ternary(ks[7], (D_HID, D_HID)), 'h2_s': jax.random.uniform(ks[8], (D_HID,), dtype=jnp.float32) * inv(D_HID), 'w3_w': _ternary(ks[9], (D_IN, D_HID)), 'w3_s': jax.random.uniform(ks[10], (D_IN,), dtype=jnp.float32) * inv(D_HID)}
    _L3_ffn_in = _L3_ffn_setup()
    _d = {'L0_attn_x': _L0_attn_in['x'], 'L0_attn_W_q': _L0_attn_in['W_q'], 'L0_attn_b_q': _L0_attn_in['b_q'], 'L0_attn_W_k': _L0_attn_in['W_k'], 'L0_attn_b_k': _L0_attn_in['b_k'], 'L0_attn_W_v': _L0_attn_in['W_v'], 'L0_attn_b_v': _L0_attn_in['b_v'], 'L0_attn_W_o': _L0_attn_in['W_o'], 'L0_attn_b_o': _L0_attn_in['b_o'], 'L0_attn_rel_k_table': _L0_attn_in['rel_k_table'], 'L0_attn_rel_v_table': _L0_attn_in['rel_v_table'], 'L0_ffn_router_w': _L0_ffn_in['router_w'], 'L0_ffn_router_b': _L0_ffn_in['router_b'], 'L0_ffn_w1': _L0_ffn_in['w1'], 'L0_ffn_w3': _L0_ffn_in['w3'], 'L0_ffn_w2': _L0_ffn_in['w2'], 'L1_attn_Wqkv': _L1_attn_in['Wqkv'], 'L1_attn_bqkv': _L1_attn_in['bqkv'], 'L1_attn_Wout': _L1_attn_in['Wout'], 'L1_attn_bout': _L1_attn_in['bout'], 'L1_ffn_w12': _L1_ffn_in['w12'], 'L1_ffn_w3': _L1_ffn_in['w3'], 'L1_ffn_gate_w': _L1_ffn_in['gate_w'], 'L2_attn_Wqkv': _L2_attn_in['Wqkv'], 'L2_attn_bqkv': _L2_attn_in['bqkv'], 'L2_attn_Wproj': _L2_attn_in['Wproj'], 'L2_attn_bproj': _L2_attn_in['bproj'], 'L2_attn_mapping': _L2_attn_in['mapping'], 'L2_ffn_W_exp': _L2_ffn_in['W_exp'], 'L2_ffn_b_exp': _L2_ffn_in['b_exp'], 'L2_ffn_up_weights': _L2_ffn_in['up_weights'], 'L2_ffn_up_bias': _L2_ffn_in['up_bias'], 'L2_ffn_down_weights': _L2_ffn_in['down_weights'], 'L2_ffn_W_con': _L2_ffn_in['W_con'], 'L2_ffn_b_con': _L2_ffn_in['b_con'], 'L2_ffn_down_bias': _L2_ffn_in['down_bias'], 'L3_attn_Wq': _L3_attn_in['Wq'], 'L3_attn_Wk': _L3_attn_in['Wk'], 'L3_attn_Wv': _L3_attn_in['Wv'], 'L3_attn_Wo': _L3_attn_in['Wo'], 'L3_attn_bo': _L3_attn_in['bo'], 'L3_attn_planes_T': _L3_attn_in['planes_T'], 'L3_attn_protos_T': _L3_attn_in['protos_T'], 'L3_attn_logit_temp': _L3_attn_in['logit_temp'], 'L3_ffn_w1_w': _L3_ffn_in['w1_w'], 'L3_ffn_w1_s': _L3_ffn_in['w1_s'], 'L3_ffn_w2_w': _L3_ffn_in['w2_w'], 'L3_ffn_w2_s': _L3_ffn_in['w2_s'], 'L3_ffn_h1_w': _L3_ffn_in['h1_w'], 'L3_ffn_h1_s': _L3_ffn_in['h1_s'], 'L3_ffn_h2_w': _L3_ffn_in['h2_w'], 'L3_ffn_h2_s': _L3_ffn_in['h2_s'], 'L3_ffn_w3_w': _L3_ffn_in['w3_w'], 'L3_ffn_w3_s': _L3_ffn_in['w3_s']}
    _x0 = _d['L0_attn_x']
    _d['L0_attn_x'] = jax.random.normal(jax.random.fold_in(jax.random.key(seed), 1), (16, 256, 128), dtype=_x0.dtype)
    del _x0
    return _d

def reference(L0_attn_x, L0_attn_W_q, L0_attn_b_q, L0_attn_W_k, L0_attn_b_k, L0_attn_W_v, L0_attn_b_v, L0_attn_W_o, L0_attn_b_o, L0_attn_rel_k_table, L0_attn_rel_v_table, L0_ffn_router_w, L0_ffn_router_b, L0_ffn_w1, L0_ffn_w3, L0_ffn_w2, L1_attn_Wqkv, L1_attn_bqkv, L1_attn_Wout, L1_attn_bout, L1_ffn_w12, L1_ffn_w3, L1_ffn_gate_w, L2_attn_Wqkv, L2_attn_bqkv, L2_attn_Wproj, L2_attn_bproj, L2_attn_mapping, L2_ffn_W_exp, L2_ffn_b_exp, L2_ffn_up_weights, L2_ffn_up_bias, L2_ffn_down_weights, L2_ffn_W_con, L2_ffn_b_con, L2_ffn_down_bias, L3_attn_Wq, L3_attn_Wk, L3_attn_Wv, L3_attn_Wo, L3_attn_bo, L3_attn_planes_T, L3_attn_protos_T, L3_attn_logit_temp, L3_ffn_w1_w, L3_ffn_w1_s, L3_ffn_w2_w, L3_ffn_w2_s, L3_ffn_h1_w, L3_ffn_h1_s, L3_ffn_h2_w, L3_ffn_h2_s, L3_ffn_w3_w, L3_ffn_w3_s):

    def _L0_attn_ref(x, W_q, b_q, W_k, b_k, W_v, b_v, W_o, b_o, rel_k_table, rel_v_table):
        import jax, jax.numpy as jnp
        import numpy as np
        EMBED_DIM = 128
        NUM_HEADS = 16
        HEAD_DIM = EMBED_DIM // NUM_HEADS
        SEQ_LEN = 128
        BATCH = 4
        MAX_REL_POS = 2

        def _rel_index(length_q, length_k):
            q = jnp.arange(length_q)[:, None]
            k = jnp.arange(length_k)[None, :]
            return jnp.clip(k - q, -MAX_REL_POS, MAX_REL_POS) + MAX_REL_POS
        B, S, E = x.shape
        H, D = (NUM_HEADS, HEAD_DIM)
        scale = jnp.sqrt(jnp.asarray(D, x.dtype))
        Q = x @ W_q + b_q
        K = x @ W_k + b_k
        V = x @ W_v + b_v
        Qh = Q.reshape(B, S, H, D).transpose(0, 2, 1, 3)
        Kh = K.reshape(B, S, H, D).transpose(0, 2, 1, 3)
        Vh = V.reshape(B, S, H, D).transpose(0, 2, 1, 3)
        scores = jnp.einsum('bhqd,bhkd->bhqk', Qh, Kh)
        idx = _rel_index(S, S)
        rel_k = rel_k_table[idx]
        scores = (scores + jnp.einsum('bhqd,qkd->bhqk', Qh, rel_k)) / scale
        causal = jnp.tril(jnp.ones((S, S), dtype=bool))
        scores = jnp.where(causal[None, None], scores, jnp.asarray(-1000000000.0, scores.dtype))
        attn = jax.nn.softmax(scores, axis=-1)
        out = jnp.einsum('bhqk,bhkd->bhqd', attn, Vh)
        rel_v = rel_v_table[idx]
        out = out + jnp.einsum('bhqk,qkd->bhqd', attn, rel_v)
        out = out.transpose(0, 2, 1, 3).reshape(B, S, E)
        return out @ W_o + b_o

    def _L0_ffn_ref(x, router_w, router_b, w1, w3, w2):
        import jax, jax.numpy as jnp
        import numpy as np
        B, S, D, F, E, K = (4, 256, 128, 512, 4, 2)
        b, s, d = x.shape
        T = b * s
        e = router_w.shape[1]
        xf = x.reshape(T, d)
        logits = xf @ router_w + router_b
        probs = jax.nn.softmax(logits, axis=-1)
        top_p, top_i = jax.lax.top_k(probs, K)
        top_p = top_p / jnp.sum(top_p, axis=-1, keepdims=True)
        gates = jnp.zeros((T, e), xf.dtype).at[jnp.arange(T)[:, None], top_i].add(top_p)
        h = jax.nn.silu(jnp.einsum('td,edf->etf', xf, w1)) * jnp.einsum('td,edf->etf', xf, w3)
        expert_out = jnp.einsum('etf,efd->etd', h, w2)
        out = jnp.einsum('te,etd->td', gates, expert_out)
        return out.reshape(b, s, d)

    def _L1_attn_ref(x, Wqkv, bqkv, Wout, bout):
        import jax, jax.numpy as jnp
        import numpy as np
        H = 16
        WIN = 64
        B, S, D = x.shape
        d = D // H
        pads = WIN // 2
        C = WIN
        N = S // C
        L = C + WIN - 1
        qkv = (x @ Wqkv.T + bqkv).reshape(B, S, 3, H, d).transpose(2, 0, 3, 1, 4)
        q, k, v = (qkv[0], qkv[1], qkv[2])
        kp = jnp.pad(k, ((0, 0), (0, 0), (pads, pads), (0, 0)))
        vp = jnp.pad(v, ((0, 0), (0, 0), (pads, pads), (0, 0)))
        idx = jnp.arange(N)[:, None] * C + jnp.arange(L)[None, :]
        kb = kp[:, :, idx, :]
        vb = vp[:, :, idx, :]
        qc = q.reshape(B, H, N, C, d)
        scores = jnp.einsum('bhncd,bhnld->bhncl', qc, kb) / np.sqrt(d).astype(np.float32)
        c = jnp.arange(C)[:, None]
        j = jnp.arange(L)[None, :]
        band = (j >= c) & (j < c + WIN)
        scores = jnp.where(band, scores, -jnp.inf)
        attn = jax.nn.softmax(scores, axis=-1)
        o = jnp.einsum('bhncl,bhnld->bhncd', attn, vb).reshape(B, H, S, d)
        o = o.transpose(0, 2, 1, 3).reshape(B, S, D)
        return o @ Wout.T + bout

    def _L1_ffn_ref(x, w12, w3, gate_w):
        import jax, jax.numpy as jnp
        import numpy as np
        TOP_K = 2
        E = gate_w.shape[0]
        H = w3.shape[-1]
        scores = jnp.einsum('btd,ed->bte', x, gate_w)
        topk_scores, topk_idx = jax.lax.top_k(scores, TOP_K)
        topk_probs = jax.nn.softmax(topk_scores, axis=-1)
        total_probs = jnp.sum(jax.nn.one_hot(topk_idx, E, dtype=topk_probs.dtype) * topk_probs[..., None], axis=-2)
        h12 = jnp.einsum('btd,ehd->bteh', x, w12)
        h1, h2 = (h12[..., :H], h12[..., H:])
        hidden = jax.nn.silu(h1) * h2
        expert_out = jnp.einsum('bteh,edh->bted', hidden, w3)
        y = jnp.sum(total_probs[..., None] * expert_out, axis=-2)
        return y

    def _L2_attn_ref(x, Wqkv, bqkv, Wproj, bproj, mapping):
        import jax, jax.numpy as jnp
        import numpy as np
        import math
        HEADS = 16
        SEG = 32
        DIL = 4
        BLOCK_M = 64

        def _hilbert_points(level, x=0, y=0, xi=1, xj=0, yi=0, yj=1):
            if level <= 0:
                yield (x, y)
            else:
                for pt in _hilbert_points(level - 1, x, y, yi // 2, yj // 2, xi // 2, xj // 2):
                    yield pt
                for pt in _hilbert_points(level - 1, x + xi // 2, y + xj // 2, xi // 2, xj // 2, yi // 2, yj // 2):
                    yield pt
                for pt in _hilbert_points(level - 1, x + xi // 2 + yi // 2, y + xj // 2 + yj // 2, xi // 2, xj // 2, yi // 2, yj // 2):
                    yield pt
                for pt in _hilbert_points(level - 1, x + xi // 2 + yi, y + xj // 2 + yj, -yi // 2, -yj // 2, -xi // 2, -xj // 2):
                    yield pt

        def create_hilbert_mapping(seq_len):
            grid = 2 ** int(math.ceil(math.log2(math.sqrt(seq_len))))
            pts = list(_hilbert_points(int(math.log2(grid)), 0, 0, grid, 0, 0, grid))
            m = np.zeros(seq_len, dtype=np.int32)
            for hidx, (x, y) in enumerate(pts[:seq_len]):
                lin = y * grid + x
                if lin < seq_len:
                    m[lin] = hidx
            return jnp.asarray(m)

        def _hilbert_attention(x, Wqkv, bqkv, Wproj, bproj, mapping):
            B, M, dim = x.shape
            H = HEADS
            D = dim // H
            scale = D ** (-0.5)
            qkv = (x @ Wqkv + bqkv).reshape(B, M, 3, H, D)
            qkv = jnp.transpose(qkv, (2, 0, 3, 1, 4))
            q, k, v = (qkv[0], qkv[1], qkv[2])
            nb = M // BLOCK_M
            rm = jnp.arange(M).reshape(nb, BLOCK_M)
            mrm = mapping[rm].astype(jnp.int32)
            seg_idx = mrm // SEG
            offs = jnp.arange(0, SEG, DIL)
            key_pos = seg_idx[:, :, None] * SEG + offs[None, None, :]
            mask_k = key_pos < M
            kp0 = key_pos[:, 0, :]
            mask0 = mask_k[:, 0, :]
            idx0 = jnp.where(mask0, mapping[jnp.clip(kp0, 0, M - 1)], 0)
            Ksel = k[:, :, idx0, :] * mask0[None, None, :, :, None]
            Vsel = v[:, :, idx0, :] * mask0[None, None, :, :, None]
            qm = q[:, :, mrm, :] * scale
            scores = jnp.einsum('bhnmd,bhnsd->bhnms', qm, Ksel)
            scores = jnp.where(mask_k[None, None], scores, -1000000000.0)
            sexp = jnp.exp(scores - jnp.max(scores, axis=3, keepdims=True))
            acc = jnp.einsum('bhnms,bhnsd->bhnmd', sexp, Vsel)
            lsum = 1e-06 + jnp.sum(sexp, axis=-1)
            out = acc / lsum[..., None]
            out = out.reshape(B, H, M, D).transpose(0, 2, 1, 3).reshape(B, M, dim)
            return out @ Wproj + bproj
        return _hilbert_attention(x, Wqkv, bqkv, Wproj, bproj, mapping)

    def _L2_ffn_ref(x, W_exp, b_exp, up_weights, up_bias, down_weights, W_con, b_con, down_bias):
        import jax, jax.numpy as jnp
        import numpy as np
        D_MODEL = 128
        EXPANSION = 4
        D_HIDDEN = D_MODEL * EXPANSION
        NUM_STAGES = int(np.log2(D_HIDDEN))

        def butterfly(y, weights, dim):
            lead = y.shape[:-1]
            for stage in range(weights.shape[0]):
                s = 2 ** stage
                nb = dim // (2 * s)
                yr = y.reshape(*lead, nb, 2, s)
                a = yr[..., 0, :]
                b = yr[..., 1, :]
                w = weights[stage].reshape(nb, s, 2, 2)
                na = w[..., 0, 0] * a + w[..., 0, 1] * b
                nb2 = w[..., 1, 0] * a + w[..., 1, 1] * b
                y = jnp.stack([na, nb2], axis=-2).reshape(*lead, dim)
            return y
        h = jnp.einsum('bsd,dh->bsh', x, W_exp) + b_exp
        h = butterfly(h, up_weights, D_HIDDEN)
        h = jax.nn.gelu(h + up_bias, approximate=False)
        h = butterfly(h, down_weights, D_HIDDEN)
        y = jnp.einsum('bsh,hd->bsd', h, W_con) + b_con
        return y + down_bias

    def _L3_attn_ref(x, Wq, Wk, Wv, Wo, bo, planes_T, protos_T, logit_temp):
        import jax, jax.numpy as jnp
        import numpy as np
        D_K, HEADS, K_BITS, L_TABLES = (128, 16, 4, 8)
        HEAD_DIM = D_K // HEADS
        R = 1 << K_BITS
        S = L_TABLES * R
        B, T = (4, 512)

        def _protos_T():
            r = np.arange(R)
            bits = r[:, None] >> K_BITS - 1 - np.arange(K_BITS) & 1
            corners = (2.0 * bits - 1.0).astype(np.float32)
            return jnp.asarray(corners.T)
        Bx, Tx, D = x.shape
        dim = planes_T.shape[0]
        H = D // dim
        k_bits, r = protos_T.shape
        l_tables = planes_T.shape[1] // k_bits
        s = l_tables * r

        def heads(W):
            return (x @ W.T).reshape(Bx, Tx, H, dim).transpose(0, 2, 1, 3)
        Q, K, V = (heads(Wq), heads(Wk), heads(Wv))
        scale = jnp.clip(jnp.exp(logit_temp), 0.01, 20.0)
        projK = jnp.einsum('bhtd,dp->bhtp', K, planes_T).reshape(Bx, H, Tx, l_tables, k_bits)
        logitsK = jnp.einsum('bhtlk,kr->bhtlr', jnp.tanh(projK) / scale, protos_T)
        probsK = jax.nn.softmax(logitsK, axis=-1).reshape(Bx, H, Tx, s)
        bucket_K = jnp.einsum('bhts,bhtd->bhsd', probsK, K)
        bucket_V = jnp.einsum('bhts,bhtd->bhsd', probsK, V)
        scores = jnp.einsum('bhtd,bhsd->bhts', Q, bucket_K) / jnp.sqrt(jnp.float32(dim))
        attn = jax.nn.softmax(scores, axis=-1)
        out = jnp.einsum('bhts,bhsd->bhtd', attn, bucket_V)
        out = out.transpose(0, 2, 1, 3).reshape(Bx, Tx, D)
        return out @ Wo.T + bo

    def _L3_ffn_ref(x, w1_w, w1_s, w2_w, w2_s, h1_w, h1_s, h2_w, h2_s, w3_w, w3_s):
        import jax, jax.numpy as jnp
        import numpy as np
        D_IN, D_HID = (128, 512)

        def _ternary(key, shape):
            return jax.random.randint(key, shape, -1, 2).astype(jnp.float32)

        def _tlin(x, w, s):
            return jnp.einsum('bsi,oi->bso', x, w) * s
        h = jax.nn.silu(_tlin(x, w1_w, w1_s)) * _tlin(x, w2_w, w2_s)
        h = jax.nn.gelu(_tlin(h, h1_w, h1_s), approximate=False)
        h = jax.nn.gelu(_tlin(h, h2_w, h2_s), approximate=False)
        return _tlin(h, w3_w, w3_s)
    x = L0_attn_x
    x = _layernorm(x + _L0_attn_ref(x, L0_attn_W_q, L0_attn_b_q, L0_attn_W_k, L0_attn_b_k, L0_attn_W_v, L0_attn_b_v, L0_attn_W_o, L0_attn_b_o, L0_attn_rel_k_table, L0_attn_rel_v_table), axis=-1)
    x = _layernorm(x + _L0_ffn_ref(x, L0_ffn_router_w, L0_ffn_router_b, L0_ffn_w1, L0_ffn_w3, L0_ffn_w2), axis=-1)
    x = _layernorm(x + _L1_attn_ref(x, L1_attn_Wqkv, L1_attn_bqkv, L1_attn_Wout, L1_attn_bout), axis=-1)
    x = _layernorm(x + _L1_ffn_ref(x, L1_ffn_w12, L1_ffn_w3, L1_ffn_gate_w), axis=-1)
    x = _layernorm(x + _L2_attn_ref(x, L2_attn_Wqkv, L2_attn_bqkv, L2_attn_Wproj, L2_attn_bproj, L2_attn_mapping), axis=-1)
    x = _layernorm(x + _L2_ffn_ref(x, L2_ffn_W_exp, L2_ffn_b_exp, L2_ffn_up_weights, L2_ffn_up_bias, L2_ffn_down_weights, L2_ffn_W_con, L2_ffn_b_con, L2_ffn_down_bias), axis=-1)
    x = _layernorm(x + _L3_attn_ref(x, L3_attn_Wq, L3_attn_Wk, L3_attn_Wv, L3_attn_Wo, L3_attn_bo, L3_attn_planes_T, L3_attn_protos_T, L3_attn_logit_temp), axis=-1)
    x = _layernorm(x + _L3_ffn_ref(x, L3_ffn_w1_w, L3_ffn_w1_s, L3_ffn_w2_w, L3_ffn_w2_s, L3_ffn_h1_w, L3_ffn_h1_s, L3_ffn_h2_w, L3_ffn_h2_s, L3_ffn_w3_w, L3_ffn_w3_s), axis=-1)
    return x

_drawn_inputs = setup_inputs


def setup_inputs(seed=0):
    import zlib

    import numpy as np

    out = dict(_drawn_inputs(seed))
    spreads = {'L0_attn_b_q': (0.0, 0.1),
     'L0_attn_b_k': (0.0, 0.8),
     'L0_attn_b_v': (0.0, 0.1),
     'L0_attn_b_o': (0.0, 0.1),
     'L0_ffn_router_b': (0.0, 0.8),
     'L1_attn_bqkv': (0.0, 0.1),
     'L1_attn_bout': (0.0, 0.1),
     'L2_ffn_b_exp': (0.0, 0.1),
     'L2_ffn_up_bias': (0.0, 0.1),
     'L2_ffn_b_con': (0.0, 0.1),
     'L2_ffn_down_bias': (0.0, 0.1),
     'L3_attn_bo': (0.0, 0.1)}
    factors = {'L0_ffn_w3': 2.72,
     'L2_attn_bqkv': 6.229,
     'L2_attn_bproj': 5.073,
     'L3_attn_protos_T': 2.988,
     'L3_ffn_w1_w': 8.0,
     'L3_ffn_w1_s': 8.0,
     'L3_ffn_w2_w': 8.0,
     'L3_ffn_w2_s': 8.0,
     'L3_ffn_h1_w': 8.0,
     'L3_ffn_h1_s': 8.0,
     'L3_ffn_h2_w': 8.0,
     'L3_ffn_h2_s': 8.0,
     'L3_ffn_w3_w': 8.0,
     'L3_ffn_w3_s': 8.0}
    for name, (base, spread) in spreads.items():
        noise = np.random.default_rng([zlib.crc32(name.encode()), seed]).standard_normal(out[name].shape)
        drawn = base * np.exp(spread * noise) if base else spread * noise
        out[name] = jnp.asarray(drawn.astype(out[name].dtype))
    for name, factor in factors.items():
        out[name] = (out[name] * factor).astype(out[name].dtype)
    return out
```

```python
from contextlib import ExitStack

import concourse.bass as bass
from concourse import mybir

ALU = mybir.AluOpType
ACT = mybir.ActivationFunctionType
F32 = mybir.dt.float32
F32R = mybir.dt.float32r
BF16 = mybir.dt.bfloat16
I32 = mybir.dt.int32
AX_X = mybir.AxisListType.X

P = 128
SEQ = 256
TILES = 4
GT = P * TILES
H = 16
DH = P // H
EPS = 1e-5
NEG = -1.0e9


class Core:

    def __init__(self, nc, ctx, groups):
        self.nc, self.ctx, self.groups = nc, ctx, groups
        self.phase_sems = []
        self.x_tok = self.sbuf(ctx, "x_tok", [P, groups * TILES, P])
        self.x_feat = self.sbuf(ctx, "x_feat", [P, groups * GT])
        self.xr = self.sbuf(ctx, "xr", [P, 2, TILES, P])
        self.xg = self.sbuf(ctx, "xg", [P, 2, GT + 8])
        self.xn = self.sbuf(ctx, "xn", [P, 2, TILES, P])
        self.xnf = self.sbuf(ctx, "xnf", [P, 2, GT])
        self.acc = self.sbuf(ctx, "acc", [P, TILES, P])
        self.stats = self.sbuf(ctx, "stats", [P, TILES, 6])
        self.meanvar = self.sbuf(ctx, "meanvar", [P, TILES, 2])
        self.var_eps = self.sbuf(ctx, "var_eps", [P, TILES])
        self.rstd = self.sbuf(ctx, "rstd", [P, TILES])
        self.eps = self.sbuf(ctx, "eps", [P, TILES])
        self.minus_half = self.sbuf(ctx, "minus_half", [P, TILES])
        self.ident = self.sbuf(ctx, "ident", [P, P])
        self.identb = self.sbuf(ctx, "identb", [P, P], BF16)
        self.ones_row = self.sbuf(ctx, "ones_row", [1, P])
        self.bank = ctx.enter_context(nc.psum_tensor("bank", [P, 8, 512], F32))

    def sbuf(self, ctx, name, shape, dt=F32):
        return ctx.enter_context(self.nc.sbuf_tensor(name, shape, dt))

    def sem(self, ctx, name):
        handle = self.nc.alloc_semaphore(name=name)
        if ctx is not self.ctx:
            self.phase_sems.append(handle)
        return handle

    def end_phase(self):
        self.nc.clear_and_free_semaphores(self.phase_sems)
        self.phase_sems = []
        with self.nc.Block() as block:
            @block.gpsimd
            def _(pool):
                pass


def for_groups(eng, groups, body):
    body(0, 0)
    body(0, 1)
    if groups > 2:
        with eng.Fori(1, groups // 2) as it:
            body(it, 0)
            body(it, 1)


def first(it, u):
    return isinstance(it, int) and it == 0 and u == 0


def peeled(it):
    return isinstance(it, int) and it == 0


class Chain:

    def __init__(self, eng, sem, per, missing=0):
        self.eng, self.sem, self.per, self.missing = eng, sem, per, missing
        self.n, self.base, self.want = 0, 0, 0

    def begin(self, it, u):
        short = first(it, u)
        self.n = 0
        self.base = 0 if short else (it * 2 + u) * self.per - self.missing
        self.want = self.per - (self.missing if short else 0)

    def link(self, ins):
        self.n += 1
        ins.then_inc(self.sem, 1)
        self.eng.wait_ge(self.sem, self.base + self.n)

    def end(self):
        assert self.n == self.want, f"chain: {self.n} links, not {self.want}"


class Frame:

    LN_LINKS = 1

    def __init__(self, core, ctx, name, out=None):
        self.core, self.out = core, out
        sem = lambda n: core.sem(ctx, f"{name}_{n}")
        self.x_loaded = [sem("x_loaded0"), sem("x_loaded1")]
        self.x_stored = [sem("x_stored0"), sem("x_stored1")]
        self.norm_stats = sem("norm_stats")
        self.norm_eps = sem("norm_eps")
        self.norm_rstd = sem("norm_rstd")
        self.norm_done = sem("norm_done")
        self.turned = sem("turned")
        self.turned_out = sem("turned_out")
        self.stores = 16 if out is not None else 32

    def load(self, eng, it, u, group_used, used_per_group):
        core, g = self.core, it * 2 + u
        feat = core.x_feat[:, bass.ds(g * GT, GT)] if not peeled(it) else core.x_feat[:, g * GT:(g + 1) * GT]
        tok = core.x_tok[:, bass.ds(g * TILES, TILES), :] if not peeled(it) else core.x_tok[:, g * TILES:(g + 1) * TILES, :]
        if not peeled(it):
            loads, used, normed = eng.to_reg(it * 32), eng.to_reg((it * 2 + (u - 1)) * used_per_group), eng.to_reg(it * 2 + (u - 1))
            eng.wait_ge(self.x_loaded[u], loads)
            eng.wait_ge(group_used, used)
            eng.wait_ge(self.norm_done, normed)
        eng.dma_start(core.xg[:, u, 8:], feat).then_inc(self.x_loaded[u], 16)
        eng.dma_start(core.xr[:, u], tok).then_inc(self.x_loaded[u], 16)

    def wait_loaded(self, eng, it, u):
        eng.wait_ge(self.x_loaded[u], (it + 1) * 32)

    def norm(self, nc, dve, chain, it, u):
        core, g = self.core, it * 2 + u
        for t in range(TILES):
            last = dve.bn_stats(core.stats[:, t, :], core.acc[:, t, :])
        chain.link(last)
        dve.nop(nofuse=True)
        for t in range(TILES):
            last = dve.bn_aggr(core.meanvar[:, t, :], core.stats[:, t, :])
        last.then_inc(self.norm_stats, 1)
        dve.wait_ge(self.norm_rstd, g + 1)
        if not peeled(it):
            dve.wait_ge(self.x_stored[u], it * self.stores + 1)
        for t in range(TILES):
            last = dve.tensor_scalar(core.xn[:, u, t, :], core.acc[:, t, :], core.meanvar[:, t, 0:1],
                                     core.rstd[:, t:t + 1], ALU.subtract, ALU.mult)
        last.then_inc(self.norm_done, 1)
        dve.wait_ge(self.norm_done, g + 1)

    def pool(self, eng):
        for_groups(eng, self.core.groups, lambda it, u: self.pool_group(eng, it, u))

    def pool_group(self, eng, it, u):
        core, g = self.core, it * 2 + u
        eng.wait_ge(self.norm_stats, g + 1)
        if not first(it, u):
            eng.wait_ge(self.norm_done, g)
        eng.tensor_tensor(core.var_eps[:], core.meanvar[:, :, 1], core.eps[:], ALU.add).then_inc(self.norm_eps, 1)
        eng.wait_ge(self.norm_eps, g + 1)
        eng.tensor_tensor(core.rstd[:], core.var_eps[:], core.minus_half[:], ALU.pow).then_inc(self.norm_rstd, 1)

    def turn(self, pe, bank, it, u):
        if self.out is not None:
            return
        core, g = self.core, it * 2 + u
        pe.wait_ge(self.norm_done, g + 1)
        if not first(it, u):
            pe.wait_ge(self.turned_out, g)
        for t in range(TILES):
            last = pe.transpose(core.bank[:, bank, t * P:(t + 1) * P], core.xn[:, u, t, :], core.ident[:])
        last.then_inc(self.turned, 1)

    def begin(self, act):
        for u in range(2):
            act.sem_inc(self.x_stored[u], 1)

    def store(self, act, bank, it, u):
        core, g = self.core, it * 2 + u
        tiles = bass.ds(g * TILES, TILES) if not peeled(it) else slice(g * TILES, (g + 1) * TILES)
        cols = bass.ds(g * GT, GT) if not peeled(it) else slice(g * GT, (g + 1) * GT)
        if self.out is not None:
            act.wait_ge(self.norm_done, g + 1)
            act.dma_start(self.out[:, tiles, :], core.xn[:, u]).then_inc(self.x_stored[u], 16)
            return
        act.wait_ge(self.turned, g + 1)
        if not peeled(it):
            act.wait_ge(self.x_stored[u], it * 32 + 1)
        act.copy(core.xnf[:, u, :], core.bank[:, bank, :]).then_inc(self.turned_out, 1)
        act.dma_start(core.x_tok[:, tiles, :], core.xn[:, u]).then_inc(self.x_stored[u], 16)
        act.wait_ge(self.turned_out, g + 1)
        act.dma_start(core.x_feat[:, cols], core.xnf[:, u, :]).then_inc(self.x_stored[u], 16)

    def previous(self, it, u):
        return (it, 0) if u else (it - 1, 1)

    def finish(self, eng):
        for u in range(2):
            eng.wait_ge(self.x_stored[u], self.core.groups // 2 * self.stores + 1)


def setup(core, D, params):
    nc, groups = core.nc, core.groups
    with ExitStack() as ctx:
        x_in = core.sem(ctx, "x_in")
        ident_in = core.sem(ctx, "ident_in")
        const = core.sem(ctx, "setup_const")
        turned = core.sem(ctx, "setup_turned")
        out = core.sem(ctx, "setup_out")
        half = core.sem(ctx, "setup_half")
        with nc.Block() as block:
            @block.sync
            def _(sp):
                sp.dma_start(core.x_tok[:], D["x"].rearrange("(t p) d -> p t d", p=P)).then_inc(x_in, 16)
                for tile, name in params:
                    sp.dma_start(tile, D[name]).then_inc(core.params_in, 16)
                sp.wait_ge(core.params_in, 16 * len(params))

            @block.gpsimd
            def _(pool):
                pool.memset(core.ident[:], 0.0).then_inc(const, 1)
                pool.wait_ge(const, 1)
                pool.affine_select(out=core.ident[:], in_=core.ident[:], compare_op=ALU.not_equal, fill=1.0,
                                   base=0, pattern=[[-1, P]], channel_multiplier=1).then_inc(ident_in, 1)
                pool.wait_ge(ident_in, 1)
                pool.tensor_copy(core.identb[:], core.ident[:])

            @block.vector
            def _(dve):
                dve.memset(core.minus_half[:], -0.5)
                dve.memset(core.eps[:], EPS)
                dve.memset(core.ones_row[:], 1.0)
                dve.memset(core.xg[:, :, 0:8], 0.0)
                for g in range(0, groups, 2):
                    dve.wait_ge(turned, g + 1)
                    dve.tensor_copy(core.x_feat[:, g * GT:(g + 1) * GT], core.bank[:, 0, :]).then_inc(out, 1)

            @block.scalar
            def _(act):
                for g in range(1, groups, 2):
                    act.wait_ge(turned, g + 1)
                    act.copy(core.x_feat[:, g * GT:(g + 1) * GT], core.bank[:, 1, :]).then_inc(half, 1)

            @block.tensor
            def _(pe):
                pe.wait_ge(x_in, 16)
                pe.wait_ge(ident_in, 1)
                for g in range(groups):
                    if g >= 2:
                        pe.wait_ge(half if g % 2 else out, g // 2)
                    for t in range(TILES):
                        last = pe.transpose(core.bank[:, g % 2, t * P:(t + 1) * P],
                                            core.x_tok[:, g * TILES + t, :], core.ident[:])
                    last.then_inc(turned, 1)


def moe(core, name, w1, w3, w2, router, router_bias, experts, out=None):
    nc, bank = core.nc, core.bank
    STEPS = 16
    FT = STEPS // experts
    E = experts
    UP1, UP3, DOWN, LOGITS, TURN = 0, 2, 4, 6, 7
    with ExitStack() as ctx:
        frame = Frame(core, ctx, name, out)
        sem = lambda n: core.sem(ctx, f"{name}_{n}")
        sb = lambda n, s, d=F32: core.sbuf(ctx, f"{name}_{n}", s, d)
        logits_done, logits_read = sem("logits_done"), sem("logits_read")
        gate_sub, gate_exp = sem("gate_sub"), sem("gate_exp")
        gate_rec, gates_made = sem("gate_rec"), sem("gates_made")
        up1_done, up3_done = sem("up1_done"), sem("up3_done")
        silu_done, hid_done = sem("silu_done"), sem("hid_done")
        down_done, y_used = sem("down_done"), sem("y_used")
        dve_chain = sem("dve_chain")
        silu = sb("silu", [P, 2, GT])
        hid = sb("hid", [P, 2, GT])
        lg = sb("lg", [P, TILES, E])
        top = sb("top", [P, TILES])
        lsub = sb("lsub", [P, TILES, E])
        lexp = sb("lexp", [P, TILES, E])
        above = sb("above", [P, TILES, E, E])
        ties = sb("ties", [P, TILES, E, E])
        earlier = sb("earlier", [P, E, E])
        rank = sb("rank", [P, TILES, E])
        chosen = sb("chosen", [P, TILES, E])
        total = sb("total", [P, TILES])
        gates = sb("gates", [P, TILES, E])
        mask_made = sem("mask_made")
        logits = bank[:, LOGITS, 0:TILES * E].rearrange("p (t e) -> p t e", e=E)

        with nc.Block() as block:
            @block.sync
            def _(sp):
                for_groups(sp, core.groups, lambda it, u: frame.load(sp, it, u, up3_done, STEPS))

            @block.gpsimd
            def _(pool):
                pool.memset(earlier[:], 1.0).then_inc(mask_made, 1)
                pool.wait_ge(mask_made, 1)
                pool.affine_select(out=earlier[:], in_=earlier[:], compare_op=ALU.is_gt, fill=0.0, base=0,
                                   pattern=[[1, E], [-1, E]], channel_multiplier=0).then_inc(mask_made, 1)
                frame.pool(pool)

            @block.tensor
            def _(pe):
                pe.wait_ge(core.ffn_in, core.wide_loads)

                def down(it, u, f):
                    g, e = it * 2 + u, f // FT
                    pe.wait_ge(hid_done, g * STEPS + (f + 1))
                    if f % FT == 0 and not (peeled(it) and u * E + e < 2):
                        pe.wait_ge(y_used, g * E + (e - 1))
                    for t in range(TILES):
                        last = pe.matmul(bank[:, DOWN + e % 2, t * P:(t + 1) * P], hid[:, f % 2, t * P:(t + 1) * P],
                                         w2[:, f, :], start=(f % FT == 0 and t == 0), stop=(f % FT == FT - 1),
                                         skip_group_check=True)
                    last.then_inc(down_done, 1)

                def body(it, u):
                    g = it * 2 + u
                    xg = core.xg[:, u, 8:]
                    frame.wait_loaded(pe, it, u)
                    if not first(it, u):
                        pe.wait_ge(logits_read, g)
                    for t in range(TILES):
                        last = pe.matmul(logits[:, t, :], xg[:, t * P:(t + 1) * P], router[:], start=(t == 0),
                                         stop=router_bias is None, skip_group_check=True)
                        if router_bias is not None:
                            last = pe.matmul(logits[:, t, :], core.ones_row[:], router_bias[:], start=False,
                                             stop=True, skip_group_check=True)
                    last.then_inc(logits_done, 1)
                    for f in range(STEPS):
                        if not (peeled(it) and u * STEPS + f < 2):
                            pe.wait_ge(hid_done, g * STEPS + (f - 1))
                        pe.matmul(bank[:, UP1 + f % 2, :], w1[:, f * P:(f + 1) * P], xg, start=True,
                                  stop=True).then_inc(up1_done, 1)
                        pe.matmul(bank[:, UP3 + f % 2, :], w3[:, f * P:(f + 1) * P], xg, start=True,
                                  stop=True).then_inc(up3_done, 1)
                        if f == 4 and not first(it, u):
                            frame.turn(pe, TURN, *frame.previous(it, u))
                        if f:
                            down(it, u, f - 1)
                    down(it, u, STEPS - 1)

                for_groups(pe, core.groups, body)
                frame.turn(pe, TURN, core.groups // 2 - 1, 1)

            @block.scalar
            def _(act):
                def body(it, u):
                    g = it * 2 + u
                    for f in range(STEPS):
                        act.wait_ge(up1_done, g * STEPS + (f + 1))
                        if not (peeled(it) and u * STEPS + f < 2):
                            act.wait_ge(hid_done, g * STEPS + (f - 1))
                        act.activation(silu[:, f % 2, :], bank[:, UP1 + f % 2, :], ACT.Silu).then_inc(silu_done, 1)
                        if f == 2:
                            act.wait_ge(gate_sub, g + 1)
                            act.activation(lexp[:], lsub[:], ACT.Exp).then_inc(gate_exp, 1)
                        if f == 5 and not first(it, u):
                            frame.store(act, TURN, *frame.previous(it, u))

                frame.begin(act)
                for_groups(act, core.groups, body)
                frame.store(act, TURN, core.groups // 2 - 1, 1)
                frame.finish(act)

            @block.vector
            def _(dve):
                chain = Chain(dve, dve_chain, 9)

                def rank_experts(it, u):
                    g = it * 2 + u
                    dve.wait_ge(logits_done, g + 1)
                    chain.link(dve.tensor_copy(lg[:], logits))
                    chain.link(dve.tensor_reduce(top[:], lg[:], AX_X, ALU.max))
                    dve.tensor_tensor(lsub[:], lg[:], top[:].unsqueeze(2).to_broadcast([P, TILES, E]),
                                      ALU.subtract).then_inc(gate_sub, 1)
                    for t in range(TILES):
                        rival = lg[:, t, :].unsqueeze(1).to_broadcast([P, E, E])
                        own = lg[:, t, :].unsqueeze(2).to_broadcast([P, E, E])
                        dve.tensor_tensor(above[:, t], rival, own, ALU.is_gt)
                        last = dve.tensor_tensor(ties[:, t], rival, own, ALU.is_equal)
                    chain.link(last)
                    chain.link(dve.tensor_tensor(ties[:], ties[:], earlier[:].unsqueeze(1).to_broadcast([P, TILES, E, E]),
                                                 ALU.mult))
                    chain.link(dve.tensor_tensor(above[:], above[:], ties[:], ALU.add))
                    chain.link(dve.tensor_reduce(rank[:], above[:], AX_X, ALU.add))
                    dve.tensor_scalar(chosen[:], rank[:], 1.5, None, ALU.is_lt).then_inc(logits_read, 1)

                def make_gates(it, u):
                    g = it * 2 + u
                    dve.wait_ge(gate_exp, g + 1)
                    dve.wait_ge(logits_read, g + 1)
                    chain.link(dve.tensor_tensor(chosen[:], chosen[:], lexp[:], ALU.mult))
                    chain.link(dve.tensor_reduce(total[:], chosen[:], AX_X, ALU.add))
                    dve.reciprocal(total[:], total[:]).then_inc(gate_rec, 1)
                    dve.wait_ge(gate_rec, g + 1)
                    dve.tensor_tensor(gates[:], chosen[:], total[:].unsqueeze(2).to_broadcast([P, TILES, E]),
                                      ALU.mult).then_inc(gates_made, 1)
                    dve.wait_ge(gates_made, g + 1)

                def add_expert(it, u, e):
                    g = it * 2 + u
                    dve.wait_ge(down_done, g * STEPS + FT * (e + 1))
                    for t in range(TILES):
                        base = core.xr[:, u, t, :] if e == 0 else core.acc[:, t, :]
                        last = dve.scalar_tensor_tensor(out=core.acc[:, t, :], in0=bank[:, DOWN + e % 2, t * P:(t + 1) * P],
                                                        scalar=gates[:, t, e:e + 1], in1=base,
                                                        op0=ALU.mult, op1=ALU.add)
                    last.then_inc(y_used, 1)
                    dve.wait_ge(y_used, g * E + (e + 1))

                def body(it, u):
                    g = it * 2 + u
                    chain.begin(it, u)
                    frame.wait_loaded(dve, it, u)
                    for f in range(STEPS):
                        dve.wait_ge(silu_done, g * STEPS + (f + 1))
                        dve.wait_ge(up3_done, g * STEPS + (f + 1))
                        if not (peeled(it) and u * STEPS + f < 2):
                            dve.wait_ge(down_done, g * STEPS + (f - 1))
                        dve.tensor_tensor(hid[:, f % 2, :], silu[:, f % 2, :], bank[:, UP3 + f % 2, :],
                                          ALU.mult).then_inc(hid_done, 1)
                        if f == 0:
                            rank_experts(it, u)
                        if f == 2:
                            make_gates(it, u)
                        if f % FT == 0 and f > 2:
                            add_expert(it, u, f // FT - 1)
                        if FT == 2 and f == 3:
                            add_expert(it, u, 0)
                    add_expert(it, u, E - 1)
                    frame.norm(nc, dve, chain, it, u)
                    chain.end()

                dve.wait_ge(mask_made, 2)
                for_groups(dve, core.groups, body)


def attention_constants(core, D):
    nc = core.nc
    core.head_of = core.sbuf(core.ctx, "head_of", [P, H])
    core.stack_sel = core.sbuf(core.ctx, "stack_sel", [P, 4, 4, P], F32R)
    core.one_row = core.sbuf(core.ctx, "one_row", [P, 4])
    with ExitStack() as ctx:
        pool_step = core.sem(ctx, "const_pool_step")
        dve_step = core.sem(ctx, "const_dve_step")
        place = core.sbuf(ctx, "place", [P, 4, 4, DH])
        with nc.Block() as block:
            @block.gpsimd
            def _(pool):
                pool.memset(place[:], 0.0)
                pool.memset(core.one_row[:], 0.0)
                pool.memset(core.head_of[:], 1.0).then_inc(pool_step, 1)
                pool.wait_ge(pool_step, 1)
                pool.affine_select(out=place[:], in_=place[:], compare_op=ALU.not_equal, fill=1.0, base=0,
                                   pattern=[[-32, 4], [-DH, 4], [-1, DH]], channel_multiplier=1)
                pool.affine_select(out=core.head_of[:], in_=core.head_of[:], compare_op=ALU.is_ge, fill=0.0, base=0,
                                   pattern=[[-DH, H]], channel_multiplier=1).then_inc(pool_step, 1)
                pool.wait_ge(pool_step, 2)
                pool.affine_select(out=core.head_of[:], in_=core.head_of[:], compare_op=ALU.is_ge, fill=0.0,
                                   base=DH - 1, pattern=[[DH, H]], channel_multiplier=-1).then_inc(pool_step, 1)
                for j in range(4):
                    pool.wait_ge(pool_step, 3 + j)
                    pool.affine_select(out=core.one_row[:], in_=core.one_row[:], compare_op=ALU.not_equal, fill=1.0,
                                       base=-(32 * j + 24), pattern=[[-1, 4]], channel_multiplier=1).then_inc(pool_step, 1)

            @block.vector
            def _(dve):
                dve.memset(core.stack_sel[:].bitcast(F32), 0.0).then_inc(dve_step, 1)
                dve.wait_ge(dve_step, 1)
                dve.wait_ge(pool_step, 7)
                for part, slots in enumerate(((0, 1), (2,), (0, 2), (1,))):
                    for s in slots:
                        dve.tensor_copy(core.stack_sel[:, part].rearrange("p a (j s d) -> p a j s d", j=4, s=4)[:, :, :, s, :],
                                        place[:])


def bias_mask(pool, sem, count, tile, conditions):
    pool.memset(tile, 0.0).then_inc(sem, 1)
    for base, channel, step in conditions:
        count += 1
        pool.wait_ge(sem, count)
        pool.affine_select(out=tile, in_=tile, compare_op=ALU.is_ge, fill=NEG, base=base,
                           pattern=[[step, tile.shape[1]]], channel_multiplier=channel).then_inc(sem, 1)
    return count + 1


def attention(core, name, kind, wq, wk, wv, wo, bq, bk, bv, bo, relk=None, relv=None, lsh=None, out=None):
    nc, bank = core.nc, core.bank
    rel, is_lsh = kind == "rel", kind == "lsh"
    KEYS = P if is_lsh else SEQ
    S_BANKS = ((0, 1), (2, 3))
    P_BANKS = (4, 5)
    O_BANK, MISC = 6, 7
    SCALE = float(DH) ** -0.5
    with ExitStack() as ctx:
        frame = Frame(core, ctx, name, out)
        sem = lambda n: core.sem(ctx, f"{name}_{n}")
        sb = lambda n, s, d=F32: core.sbuf(ctx, f"{name}_{n}", s, d)
        proj_done = sem("proj_done")
        parts_hi = sem("parts_hi")
        parts_lo = sem("parts_lo")
        prods = sem("prods")
        v_out = sem("v_out")
        stack_done = sem("stack_done")
        stack_a, stack_v = sem("stack_a"), sem("stack_v")
        misc_done, misc_out = sem("misc_done"), sem("misc_out")
        s_done, max_done = sem("s_done"), sem("max_done")
        m_made, near_exp = sem("m_made"), sem("near_exp")
        p_done, exp_done, pv_done = sem("p_done"), sem("exp_done"), sem("pv_done")
        o_out = sem("o_out")
        o_turned = sem("o_turned")
        att_made = sem("att_made")
        y_done = sem("y_done")
        dve_chain = sem("dve_chain")
        pre, v_zero = sem("pre"), sem("v_zero")
        pre_pe, pre_mask, pre_act = sem("pre_pe"), sem("pre_mask"), sem("pre_act")

        wqs = sb("wqs", [P, P])
        bqs = sb("bqs", [P, 1])
        kbias = sb("kbias", [P, 1])
        NV = 3 if rel else 1
        vrows = sb("vrows", [1, NV, P])
        vb = sb("vb", [P, NV, P])
        hi = sb("hi", [P, 2, GT], F32R)
        lo = sb("lo", [P, 2, GT], F32R)
        stacks = sb("stacks", [P, 2, 4, GT], F32R)
        VSTEP = P + 2 * DH
        vpad = sb("vpad", [P, 2 if is_lsh else TILES, 2, 8 * VSTEP])
        vslot = vpad[:].rearrange("p t a (b w) -> p t a b w", w=VSTEP)
        ot = sb("ot", [P, GT])
        prob = sb("prob", [P, 2, 384])
        smax = sb("smax", [P, 2, 2, H])
        mround = sb("mround", [P, 2, H], F32R)
        mneg = sb("mneg", [P, 2, 4, 32])
        NE = 2 if rel else 1
        near = sb("near", [P, 2, NE, 2, H])
        near_e = sb("near_e", [P, 2, NE, 2, H])
        den = sb("den", [P, 2, H])
        att = sb("att", [P, 2, 2, P])
        part = sb("part", [P, 2, 2, P])
        attt = sb("attt", [P, GT])
        if rel:
            qf = sb("qf", [P, GT])
            kf = sb("kf", [P, GT + 8])
            prod = sb("prod", [P, 2, GT])
            v_near = sb("v_near", [P, 2, TILES, P])
            start_mask = sb("start_mask", [P, 2, H])
            dots = sb("dots", [P, TILES, 2, H])
            mask_q = sb("mask_q", [P, 130], BF16)
            mask_k = sb("mask_k", [P, 130], BF16)
            q_regions = [(0, 0, 128, 0, mask_q[:, 2:130]), (1, 0, 256, 126, mask_q[:])]
            k_regions = [(0, 0, 256, 0, mask_k[:]), (1, 128, 128, 0, mask_k[:, 0:128])]
        elif is_lsh:
            q_regions = [(0, 0, P, 0, None), (1, 0, P, 0, None)]
            k_regions = [(0, 0, SEQ, 0, None)]
            wkp = sb("wkp", [P, 4 * P])
            planes_bd = sb("planes_bd", [P, H, 32])
            protos_bd = sb("protos_bd", [P, 32, 16])
            group_of = sb("group_of", [P, 32])
            iscale = sb("iscale", [P, 1])
            hashed = sb("hashed", [P, 4, GT])
            kv = sb("kv", [P, TILES, H, 2 * DH])
            corner = sb("corner", [P, 2, 4 * P])
            cmax = sb("cmax", [P, 2, 32])
            csum = sb("csum", [P, 2, 32])
            weight = sb("weight", [P, 4, 4 * P])
            bkeys = sb("bkeys", [P, 2, P])
            bt = sb("bt", [P, 2, P])
            hash_done, hash_out = sem("hash_done"), sem("hash_out")
            kv_out_a, kv_out_v = sem("kv_out_a"), sem("kv_out_v")
            logit_done, logit_sub = sem("logit_done"), sem("logit_sub")
            corner_exp, corner_sum, weight_made = sem("corner_exp"), sem("corner_sum"), sem("weight_made")
            bucket_done, bucket_out = sem("bucket_done"), sem("bucket_out")
            bt_done = sem("bt_done")
            bparts = sem("bparts")
        else:
            pad_score = sb("pad_score", [P, 2, H])
            pad_count = sb("pad_count", [P, 2, H])
            masks = sb("masks", [P, 4, 160], BF16)
            q_regions = [(0, 0, 160, 0, masks[:, 0]), (1, 96, 160, 0, masks[:, 1])]
            k_regions = [(0, 0, 160, 0, masks[:, 2]), (1, 96, 160, 0, masks[:, 3])]
        NPROJ = 4 if rel else 1 if is_lsh else 3
        NHI = 4 if rel else 1 if is_lsh else 2
        NMISC = 5 if rel else 4
        MISC_AT = {"att1": 0, "dots": 1, "neg0": 1 + rel, "neg1": 2 + rel, "att0": 3 + rel}
        nq = sum(r[2] for r in q_regions)
        nk = sum(r[2] for r in k_regions)
        o_view = bank[:, MISC, :].rearrange("p (t h d) -> p t h d", t=2, h=H)

        def misc_number(it, u, what):
            return (it * 2 + u) * NMISC + (MISC_AT[what] - 1)

        MASKS = 6 if rel else 3 if is_lsh else 14

        with nc.Block() as block:
            @block.sync
            def _(sp):
                for_groups(sp, core.groups, lambda it, u: frame.load(sp, it, u, *((logit_done, 16) if is_lsh else (proj_done, NPROJ))))

            @block.gpsimd
            def _(pool):
                def lsh_pool(pool):
                    def body(it, u):
                        g = it * 2 + u
                        for n in range(16):
                            pool.wait_ge(corner_sum, g * 16 + n + 1)
                            if n >= 4:
                                pool.wait_ge(bucket_done, g * 8 + (n - 4) // 2 + 1)
                            pool.tensor_tensor(weight[:, n % 4].rearrange("p (a r) -> p a r", r=16),
                                               corner[:, n % 2].rearrange("p (a r) -> p a r", r=16),
                                               csum[:, n % 2].unsqueeze(2).to_broadcast([P, 32, 16]),
                                               ALU.mult).then_inc(weight_made, 1)
                        if not first(it, u):
                            frame.pool_group(pool, *frame.previous(it, u))

                    for_groups(pool, core.groups, body)
                    frame.pool_group(pool, core.groups // 2 - 1, 1)

                if rel:
                    pool.memset(start_mask[:], NEG).then_inc(pre_mask, 1)
                    pool.wait_ge(pre_mask, 1)
                    pool.affine_select(out=start_mask[:], in_=start_mask[:], compare_op=ALU.is_equal, fill=0.0, base=0,
                                       pattern=[[1, 2], [0, H]], channel_multiplier=1).then_inc(pre_mask, 1)
                    n = bias_mask(pool, pre_mask, 2, mask_q[:], [(0, 1, -1)])
                    n = bias_mask(pool, pre_mask, n, mask_k[:], [(-2, -1, 1)])
                elif is_lsh:
                    pool.memset(group_of[:], 1.0).then_inc(pre_mask, 1)
                    n = 1
                    for base, channel, step in ((0, 1, -4), (3, -1, 4)):
                        pool.wait_ge(pre_mask, n)
                        pool.affine_select(out=group_of[:], in_=group_of[:], compare_op=ALU.is_ge, fill=0.0, base=base,
                                           pattern=[[step, 32]], channel_multiplier=channel).then_inc(pre_mask, 1)
                        n += 1
                else:
                    pool.memset(pad_score[:], 0.0)
                    pool.iota(pad_count[:, 0, :], pattern=[[0, H]], base=32, channel_multiplier=-1,
                              allow_small_or_imprecise_dtypes=True)
                    pool.iota(pad_count[:, 1, :], pattern=[[0, H]], base=-96, channel_multiplier=1,
                              allow_small_or_imprecise_dtypes=True).then_inc(pre_mask, 1)
                    pool.wait_ge(pre_mask, 1)
                    pool.affine_select(out=pad_score[:, 0, :], in_=pad_score[:, 0, :], compare_op=ALU.is_ge, fill=NEG,
                                       base=31, pattern=[[0, H]], channel_multiplier=-1)
                    pool.affine_select(out=pad_score[:, 1, :], in_=pad_score[:, 1, :], compare_op=ALU.is_ge, fill=NEG,
                                       base=-97, pattern=[[0, H]], channel_multiplier=1)
                    pool.tensor_scalar(pad_count[:], pad_count[:], 0.0, None, ALU.max).then_inc(pre_mask, 1)
                    n = bias_mask(pool, pre_mask, 2, masks[:, 0], [(32, -1, 1), (31, 1, -1)])
                    n = bias_mask(pool, pre_mask, n, masks[:, 1], [(0, -1, 1), (63, 1, -1)])
                    n = bias_mask(pool, pre_mask, n, masks[:, 2], [(32, 1, -1), (31, -1, 1)])
                    n = bias_mask(pool, pre_mask, n, masks[:, 3], [(64, 1, -1), (-1, -1, 1)])
                assert n == MASKS
                if is_lsh:
                    lsh_pool(pool)
                else:
                    frame.pool(pool)

            @block.tensor
            def _(pe):
                pe.wait_ge(pre, 1)
                if is_lsh:
                    pe.matmul(bank[:, 0, :], wk[:], planes_bd[:].rearrange("p h n -> p (h n)"),
                              start=True, stop=True).then_inc(pre_pe, 1)
                else:
                    pe.matmul(bank[:, 0, 0:NV * P], core.ones_row[:], vrows[:].rearrange("p a b -> p (a b)"),
                              start=True, stop=True).then_inc(pre_pe, 1)
                pe.wait_ge(pre, 2)
                pe.wait_ge(pre_mask, MASKS)

                def project(it, u):
                    g = it * 2 + u
                    xg = core.xg[:, u, 8:]
                    frame.wait_loaded(pe, it, u)
                    if not first(it, u):
                        pe.wait_ge(max_done, g * 16)
                    pe.matmul(bank[:, 0, :], wqs[:], xg, start=True, stop=True).then_inc(proj_done, 1)
                    if is_lsh:
                        buckets(it, u)
                        return
                    pe.matmul(bank[:, 1, :], wk[:], xg, start=True, stop=True).then_inc(proj_done, 1)
                    for shift in range(NPROJ - 2):
                        for t in range(TILES):
                            c = 8 - shift + t * P
                            last = pe.matmul(bank[:, 2 + shift, t * P:(t + 1) * P], core.xg[:, u, c:c + P], wv[:],
                                             start=(t == 0), stop=True, skip_group_check=True)
                        last.then_inc(proj_done, 1)

                def buckets(it, u):
                    g = it * 2 + u
                    xg = core.xg[:, u, 8:]
                    for c in range(4):
                        b = (1, 2, 3, 1)[c]
                        if c == 3:
                            pe.wait_ge(hash_out, g * 4 + 1)
                        pe.matmul(bank[:, b, :], wkp[:, c * P:(c + 1) * P], xg, start=True, stop=True).then_inc(hash_done, 1)
                    if not first(it, u):
                        pe.wait_ge(exp_done, g * 32)
                    for t in range(TILES):
                        last = pe.matmul(bank[:, 4 + t // 2, (t % 2) * SEQ:(t % 2 + 1) * SEQ], xg[:, t * P:(t + 1) * P], wv[:],
                                         start=(t % 2 == 0), stop=True, skip_group_check=True)
                        last.then_inc(hash_done, 1)
                    pe.wait_ge(hash_out, g * 4 + 4)
                    pe.wait_ge(parts_lo, g * 2 + 1)
                    pe.wait_ge(kv_out_a, g + 1)
                    pe.wait_ge(kv_out_v, g + 1)

                    def sum_buckets(m):
                        s, c = m // 4, m % 4
                        pe.wait_ge(weight_made, g * 16 + 2 * m + 2)
                        for e in range(4):
                            h = 4 * c + e
                            for t in range(2):
                                last = pe.matmul(bank[:, s, h * 16:(h + 1) * 16], weight[:, (2 * m + t) % 4, e * P:(e + 1) * P],
                                                 kv[:, 2 * s + t, h, :], start=(c == 0 and e == 0 and t == 0), stop=True,
                                                 skip_group_check=True)
                        last.then_inc(bucket_done, 1)

                    for n in range(16):
                        s, c, t = n // 8, n // 2 % 4, n % 2
                        if n >= 2:
                            pe.wait_ge(logit_sub, g * 16 + n - 1)
                        pe.matmul(bank[:, 2 + n % 2, :], hashed[:, c, (2 * s + t) * P:(2 * s + t + 1) * P],
                                  protos_bd[:].rearrange("p a r -> p (a r)"), start=True, stop=True).then_inc(logit_done, 1)
                        if n % 2 and n >= 3:
                            sum_buckets(n // 2 - 1)
                    sum_buckets(7)
                    for s in range(2):
                        pe.wait_ge(bucket_out, g * 2 + s + 1)
                        last = pe.transpose(bank[:, 4, s * P:(s + 1) * P], bkeys[:, s, :], core.ident[:])
                    last.then_inc(bt_done, 1)

                def stack(it, u):
                    g = it * 2 + u
                    if not first(it, u):
                        pe.wait_ge(exp_done, g * 32)
                    for n in range(8):
                        which, a = n // 4, n % 4
                        width = slice(0, 2 * P) if is_lsh and which else slice(0, GT)
                        if n % 4 == 0:
                            pe.wait_ge(parts_lo, g * 2 + (2 if is_lsh else which + 1))
                        if n >= 2:
                            pe.wait_ge(stack_v if n % 2 else stack_a, g * 4 + n // 2)
                        pe.matmul(bank[:, P_BANKS[n % 2], width], core.stack_sel[:, 2 * which, a, :], hi[:, which, width],
                                  start=True, stop=False)
                        pe.matmul(bank[:, P_BANKS[n % 2], width], core.stack_sel[:, 2 * which + 1, a, :], lo[:, which, width],
                                  start=False, stop=True).then_inc(stack_done, 1)

                def near_dots(it, u):
                    g = it * 2 + u
                    pe.wait_ge(prods, g * 2 + 2)
                    if not first(it, u):
                        pe.wait_ge(misc_out, misc_number(it, u, "dots"))
                    for t in range(TILES):
                        for n in range(2):
                            last = pe.matmul(bank[:, MISC, (2 * t + n) * H:(2 * t + n + 1) * H], prod[:, n, t * P:(t + 1) * P],
                                             core.head_of[:], start=(t == 0 and n == 0), stop=True, skip_group_check=True)
                    last.then_inc(misc_done, 1)

                def scores_q(it, u, s, pair):
                    g = it * 2 + u
                    if pair >= 2 or s:
                        pe.wait_ge(max_done, g * 16 + (s * 8 + pair - 1))
                    for e in range(2):
                        h = 2 * pair + e
                        b, r, a = S_BANKS[pair % 2][e], 32 * (h % 4), h // 4
                        c = 0
                        for n, (qt, k0, keys, m0, mask) in enumerate(q_regions):
                            q0 = s * SEQ + qt * P
                            last = pe.matmul(bank[:, b, c:c + keys], stacks[r:r + 32, 0, a, q0:q0 + P],
                                      stacks[r:r + 32, 1, a, s * KEYS + k0:s * KEYS + k0 + keys],
                                      start=(n == 0), stop=mask is None, skip_group_check=True)
                            if mask is not None:
                                last = pe.matmul(bank[:, b, c + m0:c + m0 + mask.shape[1]], core.identb[:], mask,
                                                 start=False, stop=True, skip_group_check=True)
                            c += keys
                    last.then_inc(s_done, 1)

                def turn_max(it, u, s):
                    g, what = it * 2 + u, f"neg{s}"
                    pe.wait_ge(m_made, g * 2 + (s + 1))
                    if not first(it, u) or MISC_AT[what] > 1:
                        pe.wait_ge(misc_out, misc_number(it, u, what))
                    for t in range(2):
                        last = pe.matmul(bank[:, MISC, t * P:(t + 1) * P], mneg[:, t].rearrange("p j h -> p (j h)"),
                                         core.ident[:], start=(t == 0), stop=True, skip_group_check=True)
                    last.then_inc(misc_done, 1)

                def scores_k(it, u, s, h):
                    g = it * 2 + u
                    b, r, a = P_BANKS[h % 2], 32 * (h % 4), h // 4
                    if s or h >= 2:
                        pe.wait_ge(exp_done, g * 32 + (s * H + h - 1))
                    c = 0
                    for n, (kt, q0, queries, m0, mask) in enumerate(k_regions):
                        last = pe.matmul(bank[:, b, c:c + queries], stacks[r:r + 32, 1, a, s * KEYS + kt * P:s * KEYS + (kt + 1) * P],
                                  stacks[r:r + 32, 0, a, s * SEQ + q0:s * SEQ + q0 + queries],
                                  start=(n == 0), stop=mask is None, skip_group_check=True)
                        if mask is not None:
                            last = pe.matmul(bank[:, b, c + m0:c + m0 + mask.shape[1]], core.identb[:], mask,
                                             start=False, stop=True, skip_group_check=True)
                        c += queries
                    last.then_inc(p_done, 1)

                def weigh(it, u, s, h):
                    g = it * 2 + u
                    pe.wait_ge(exp_done, g * 32 + (s * H + h + 1))
                    if h == 0:
                        if s:
                            pe.wait_ge(o_out, g * 2 + 1)
                        elif not first(it, u):
                            pe.wait_ge(frame.turned_out if out is None else frame.norm_done, g)
                    a, b, c = h // 8, h % 8, 0
                    for n, (kt, q0, queries, _, _) in enumerate(k_regions):
                        last = pe.matmul(bank[:, O_BANK, a * SEQ + q0:a * SEQ + q0 + queries],
                                         vpad[:, s if is_lsh else 2 * s + kt, a, b * P:(b + 1) * P],
                                         prob[:, h % 2, c:c + queries], start=(h == 0 and n == 0), stop=True,
                                         skip_group_check=True)
                        c += queries
                    last.then_inc(pv_done, 1)

                def turn_o(it, u, s):
                    g = it * 2 + u
                    pe.wait_ge(o_out, g * 2 + (s + 1))
                    if s:
                        pe.wait_ge(misc_out, g * NMISC + (NMISC - 1))
                    for t in range(2):
                        for a in range(2):
                            last = pe.transpose(o_view[:, t, 8 * a:8 * a + 8, :].rearrange("p h d -> p (h d)"),
                                                ot[:, a * SEQ + t * P:a * SEQ + (t + 1) * P], core.ident[:])
                    last.then_inc(o_turned, 1)

                def turn_att(it, u, s):
                    g = it * 2 + u
                    pe.wait_ge(att_made, g * 2 + (s + 1))
                    if s:
                        pe.wait_ge(misc_out, g * NMISC + (NMISC - 1))
                    else:
                        pe.wait_ge(misc_out, misc_number(it, u, "att0"))
                    for t in range(2):
                        last = pe.transpose(bank[:, MISC, t * P:(t + 1) * P], att[:, s, t, :], core.ident[:])
                    last.then_inc(misc_done, 1)

                def output(it, u):
                    g = it * 2 + u
                    pe.wait_ge(misc_out, (g + 1) * NMISC)
                    for t in range(TILES):
                        pe.matmul(bank[:, O_BANK, t * P:(t + 1) * P], attt[:, t * P:(t + 1) * P], wo[:],
                                  start=(t == 0), stop=False, skip_group_check=True)
                        last = pe.matmul(bank[:, O_BANK, t * P:(t + 1) * P], core.ones_row[:], bo[:],
                                         start=False, stop=True, skip_group_check=True)
                    last.then_inc(y_done, 1)

                def body(it, u):
                    g = it * 2 + u
                    if is_lsh and not first(it, u):
                        turn_o(*frame.previous(it, u), 1)
                    project(it, u)
                    if not first(it, u):
                        if not is_lsh:
                            turn_o(*frame.previous(it, u), 1)
                        turn_att(*frame.previous(it, u), 1)
                    stack(it, u)
                    if rel:
                        near_dots(it, u)
                    if not first(it, u):
                        output(*frame.previous(it, u))
                    pe.wait_ge(stack_a, g * 4 + 4)
                    pe.wait_ge(stack_v, g * 4 + 4)
                    for pair in range(8):
                        scores_q(it, u, 0, pair)
                    if not first(it, u):
                        frame.turn(pe, O_BANK, *frame.previous(it, u))
                    turn_max(it, u, 0)
                    pe.wait_ge(misc_out, misc_number(it, u, "neg0") + 1)
                    pe.wait_ge(v_out, (g + 1) * (2 if is_lsh else 1))
                    for pair in range(8):
                        scores_q(it, u, 1, pair)
                        for h in (2 * pair, 2 * pair + 1):
                            scores_k(it, u, 0, h)
                            if h:
                                weigh(it, u, 0, h - 1)
                    weigh(it, u, 0, H - 1)
                    turn_max(it, u, 1)
                    pe.wait_ge(misc_out, misc_number(it, u, "neg1") + 1)
                    for h in range(H):
                        scores_k(it, u, 1, h)
                        if h == 1:
                            turn_o(it, u, 0)
                        if h == 8:
                            turn_att(it, u, 0)
                        if h:
                            weigh(it, u, 1, h - 1)
                    weigh(it, u, 1, H - 1)

                for_groups(pe, core.groups, body)
                last = (core.groups // 2 - 1, 1)
                turn_o(*last, 1)
                turn_att(*last, 1)
                output(*last)
                frame.turn(pe, O_BANK, *last)

            @block.scalar
            def _(act):
                def misc(it, u, what, out, cols):
                    number = misc_number(it, u, what) + 1 if what != "att1" else (it * 2 + u + 1) * NMISC
                    act.wait_ge(misc_done, number)
                    act.copy(out, bank[:, MISC, cols]).then_inc(misc_out, 1)

                def exps(it, u, s, h):
                    g = it * 2 + u
                    act.wait_ge(p_done, g * 32 + (s * H + h + 1))
                    if not (first(it, u) and s == 0 and h < 2):
                        act.wait_ge(pv_done, g * 32 + (s * H + h - 1))
                    act.activation(prob[:, h % 2, 0:nk], bank[:, P_BANKS[h % 2], 0:nk], ACT.Exp).then_inc(exp_done, 1)

                def hashes(it, u):
                    g = it * 2 + u
                    for c in range(4):
                        act.wait_ge(hash_done, g * 8 + c + 1)
                        act.activation(hashed[:, c, :], bank[:, (1, 2, 3, 1)[c], :], ACT.Tanh).then_inc(hash_out, 1)
                    act.wait_ge(hash_done, g * 8 + 6)
                    act.copy(kv[:, 0:2].rearrange("p t h d -> p (t h d)"), bank[:, 4, :]).then_inc(kv_out_a, 1)
                    for n in range(16):
                        act.wait_ge(logit_sub, g * 16 + n + 1)
                        act.activation(corner[:, n % 2], corner[:, n % 2], ACT.Exp).then_inc(corner_exp, 1)

                def weighed_out(it, u, s):
                    g = it * 2 + u
                    act.wait_ge(pv_done, g * 32 + (s * H + H))
                    if s or not first(it, u):
                        act.wait_ge(o_turned, g * 2 + s)
                    act.copy(ot[:], bank[:, O_BANK, :]).then_inc(o_out, 1)

                def near_exps(it, u, s):
                    g = it * 2 + u
                    act.wait_ge(m_made, g * 2 + (s + 1))
                    if not first(it, u):
                        act.wait_ge(att_made, g * 2)
                    act.activation(near_e[:, s], near[:, s], ACT.Exp).then_inc(near_exp, 1)

                def body(it, u):
                    g = it * 2 + u
                    act.wait_ge(proj_done, g * NPROJ + 1)
                    if rel:
                        if not first(it, u):
                            act.wait_ge(prods, g * 2)
                        act.activation(qf[:], bank[:, 0, :], ACT.Identity, bias=bqs[:]).then_inc(parts_hi, 1)
                    act.activation(hi[:, 0, :], bank[:, 0, :], ACT.Identity, bias=bqs[:]).then_inc(parts_hi, 1)
                    if is_lsh:
                        hashes(it, u)
                        act.wait_ge(bt_done, g + 1)
                        act.copy(hi[:, 1, 0:2 * P], bank[:, 4, 0:2 * P]).then_inc(bparts, 1)
                    else:
                        act.wait_ge(proj_done, g * NPROJ + 2)
                    if rel:
                        act.activation(kf[:, 8:], bank[:, 1, :], ACT.Identity, bias=bk[:]).then_inc(parts_hi, 1)
                    if not is_lsh:
                        act.activation(hi[:, 1, :], bank[:, 1, :], ACT.Identity, bias=kbias[:]).then_inc(parts_hi, 1)
                    for n in range(0, 8, 2):
                        if n == 4 and not first(it, u):
                            misc(*frame.previous(it, u), "att1", attt[:, SEQ:GT], slice(0, SEQ))
                        act.wait_ge(stack_done, g * 8 + n + 1)
                        width = slice(0, 2 * P) if is_lsh and n >= 4 else slice(0, GT)
                        if n < 4:
                            act.copy(stacks[:, 0, n, width], bank[:, P_BANKS[0], width]).then_inc(stack_a, 1)
                        else:
                            act.activation(stacks[:, 1, n - 4, width], bank[:, P_BANKS[0], width], ACT.Identity,
                                           bias=core.one_row[:, n - 4:n - 3]).then_inc(stack_a, 1)
                    if rel:
                        misc(it, u, "dots", dots[:].rearrange("p t n h -> p (t n h)"), slice(0, TILES * 2 * H))
                    if not first(it, u):
                        frame.store(act, O_BANK, *frame.previous(it, u))
                    if not is_lsh:
                        near_exps(it, u, 0)
                    for h in range(H):
                        exps(it, u, 0, h)
                    weighed_out(it, u, 0)
                    if not is_lsh:
                        near_exps(it, u, 1)
                    for h in range(H):
                        exps(it, u, 1, h)
                        if h == 8:
                            misc(it, u, "att0", attt[:, 0:SEQ], slice(0, SEQ))
                    weighed_out(it, u, 1)

                frame.begin(act)
                if is_lsh:
                    act.activation(iscale[:], lsh[2][:], ACT.Exp).then_inc(pre_act, 1)
                act.wait_ge(pre, 2)
                for_groups(act, core.groups, body)
                last = (core.groups // 2 - 1, 1)
                misc(*last, "att1", attt[:, SEQ:GT], slice(0, SEQ))
                frame.store(act, O_BANK, *last)
                frame.finish(act)

            @block.vector
            def _(dve):
                chain = Chain(dve, dve_chain, *((16, 5) if rel else (38, 3) if is_lsh else (12, 5)))

                pre_chain = sem("pre_chain")
                step = Chain(dve, pre_chain, 0)
                step.link(dve.tensor_scalar(wqs[:], wq[:], SCALE, None, ALU.mult))
                if not is_lsh:
                    step.link(dve.tensor_scalar(bqs[:], bq[:], SCALE, None, ALU.mult))
                if is_lsh:
                    planes, protos, temp = lsh
                    dve.wait_ge(pre_act, 1)
                    step.link(dve.memset(bqs[:], 0.0))
                    step.link(dve.tensor_scalar(iscale[:], iscale[:], 0.01, 20.0, ALU.max, ALU.min))
                    step.link(dve.reciprocal(iscale[:], iscale[:]))
                    dve.wait_ge(pre_mask, MASKS)
                    step.link(dve.tensor_tensor(protos_bd[:], protos[:].unsqueeze(1).to_broadcast([P, 32, 16]),
                                                group_of[:].unsqueeze(2).to_broadcast([P, 32, 16]), ALU.mult))
                    step.link(dve.tensor_scalar(protos_bd[:], protos_bd[:], iscale[:, 0:1], None, ALU.mult))
                    last = dve.tensor_tensor(planes_bd[:], planes[:].unsqueeze(1).to_broadcast([P, H, 32]),
                                             core.head_of[:].unsqueeze(2).to_broadcast([P, H, 32]), ALU.mult)
                elif rel:
                    step.link(dve.tensor_tensor(kbias[:], bk[:], relk[:, 0:1], ALU.add))
                    step.link(dve.memset(kf[:, 0:8], 0.0))
                    for n in range(3):
                        last = dve.tensor_tensor(vrows[:, n, :], bv[:], relv[:, n * P:(n + 1) * P], ALU.add)
                else:
                    step.link(dve.tensor_copy(kbias[:], bk[:]))
                    last = dve.tensor_copy(vrows[:, 0, :], bv[:])
                last.then_inc(pre, 1)
                dve.memset(vpad[:], 0.0).then_inc(v_zero, 1)
                dve.wait_ge(v_zero, 1)
                for t in range(vpad.shape[1]):
                    dve.memset(vslot[:, t, :, :, DH:DH + 1], 1.0)
                dve.memset(mneg[:], 0.0)
                dve.wait_ge(pre_pe, 1)
                if is_lsh:
                    dve.tensor_copy(wkp[:], bank[:, 0, :]).then_inc(pre, 1)
                else:
                    dve.tensor_copy(vb[:].rearrange("p a b -> p (a b)"), bank[:, 0, 0:NV * P]).then_inc(pre, 1)
                dve.wait_ge(pre, 2)
                dve.wait_ge(pre_mask, MASKS)

                def split(it, u):
                    g = it * 2 + u
                    for which, bias in ((0, bqs), (1, kbias)):
                        dve.wait_ge(parts_hi, g * NHI + (which + 1) * (NHI // 2))
                        dve.scalar_tensor_tensor(out=lo[:, which, :], in0=bank[:, which, :], scalar=bias[:, 0:1],
                                                 in1=hi[:, which, :].bitcast(F32), op0=ALU.add,
                                                 op1=ALU.subtract).then_inc(parts_lo, 1)
                    dve.wait_ge(proj_done, g * NPROJ + 3)
                    raw = bank[:, 2, :].rearrange("p (t d) -> p t d", t=TILES)
                    vbias = lambda n: vb[:, n, :].unsqueeze(1).to_broadcast([P, TILES, P])
                    for t in range(TILES):
                        last = dve.tensor_tensor(vslot[:, t, :, :, 0:DH],
                                                 bank[:, 2, t * P:(t + 1) * P].rearrange("p (a b d) -> p a b d", a=2, b=8),
                                                 vb[:, 0, :].rearrange("p (a b d) -> p a b d", a=2, b=8), ALU.add)
                    if rel:
                        dve.tensor_tensor(v_near[:, 0], raw, vbias(2), ALU.add)
                        dve.wait_ge(proj_done, g * NPROJ + 4)
                        last = dve.tensor_tensor(v_near[:, 1], bank[:, 3, :].rearrange("p (t d) -> p t d", t=TILES), vbias(1), ALU.add)
                    last.then_inc(v_out, 1)

                def make_buckets(it, u):
                    g = it * 2 + u
                    dve.wait_ge(parts_hi, g + 1)
                    dve.tensor_tensor(lo[:, 0, :], bank[:, 0, :], hi[:, 0, :].bitcast(F32), ALU.subtract).then_inc(parts_lo, 1)
                    dve.wait_ge(hash_done, g * 8 + 8)
                    dve.tensor_copy(kv[:, 2:4].rearrange("p t h d -> p (t h d)"), bank[:, 5, :]).then_inc(kv_out_v, 1)

                    def sum_corners(n):
                        dve.wait_ge(corner_exp, g * 16 + n + 1)
                        chain.link(dve.tensor_reduce(csum[:, n % 2], corner[:, n % 2].rearrange("p (a r) -> p a r", r=16),
                                                     AX_X, ALU.add))
                        dve.reciprocal(csum[:, n % 2], csum[:, n % 2]).then_inc(corner_sum, 1)

                    for n in range(16):
                        logits = bank[:, 2 + n % 2, :].rearrange("p (a r) -> p a r", r=16)
                        dve.wait_ge(logit_done, g * 16 + n + 1)
                        chain.link(dve.tensor_reduce(cmax[:, n % 2], logits, AX_X, ALU.max))
                        if n >= 2:
                            dve.wait_ge(weight_made, g * 16 + n - 1)
                        dve.tensor_tensor(corner[:, n % 2].rearrange("p (a r) -> p a r", r=16), logits,
                                          cmax[:, n % 2].unsqueeze(2).to_broadcast([P, 32, 16]),
                                          ALU.subtract).then_inc(logit_sub, 1)
                        if n:
                            sum_corners(n - 1)
                    sum_corners(15)
                    for s in range(2):
                        buckets = bank[:, s, 0:2 * P].rearrange("p (h d) -> p h d", h=H)
                        dve.wait_ge(bucket_done, g * 8 + 4 * s + 4)
                        dve.tensor_copy(bkeys[:, s].rearrange("p (h d) -> p h d", h=H), buckets[:, :, 0:DH]).then_inc(bucket_out, 1)
                        dve.tensor_copy(vslot[:, s, :, :, 0:DH],
                                        buckets[:, :, DH:2 * DH].rearrange("p (a b) d -> p a b d", a=2)).then_inc(v_out, 1)
                    dve.wait_ge(bparts, g + 1)
                    dve.tensor_tensor(lo[:, 1, 0:2 * P], bank[:, 4, 0:2 * P], hi[:, 1, 0:2 * P].bitcast(F32),
                                      ALU.subtract).then_inc(parts_lo, 1)

                def products(it, u):
                    g = it * 2 + u
                    dve.wait_ge(parts_hi, g * NHI + 4)
                    dve.scalar_tensor_tensor(out=prod[:, 0, :], in0=kf[:, 8:], scalar=relk[:, 2:3], in1=qf[:],
                                             op0=ALU.add, op1=ALU.mult).then_inc(prods, 1)
                    dve.scalar_tensor_tensor(out=prod[:, 1, :], in0=kf[:, 7:7 + GT], scalar=relk[:, 1:2], in1=qf[:],
                                             op0=ALU.add, op1=ALU.mult).then_inc(prods, 1)

                def maxima(it, u, s, pair):
                    g = it * 2 + u
                    dve.wait_ge(s_done, g * 16 + (s * 8 + pair + 1))
                    b = S_BANKS[pair % 2][0]
                    c = 0
                    for qt, _, keys, _, _ in q_regions:
                        last = dve.tensor_reduce(smax[:, s, qt, 2 * pair:2 * pair + 2], bank[:, b:b + 2, c:c + keys],
                                                 AX_X, ALU.max)
                        c += keys
                    last.then_inc(max_done, 1)

                def shifts(it, u, s):
                    g = it * 2 + u
                    dve.wait_ge(max_done, g * 16 + (s * 8 + 8))
                    tiles = slice(2 * s, 2 * s + 2)
                    if rel:
                        dve.wait_ge(misc_out, misc_number(it, u, "dots") + 1)
                        chain.link(dve.tensor_tensor(near[:, s, 0], smax[:, s], dots[:, tiles, 0, :], ALU.max))
                        chain.link(dve.tensor_tensor(near[:, s, 1], dots[:, tiles, 1, :], start_mask[:], ALU.add))
                        chain.link(dve.tensor_tensor(mround[:], near[:, s, 0], near[:, s, 1], ALU.max))
                        dve.tensor_tensor(near[:, s, 0], dots[:, tiles, 0, :], mround[:].bitcast(F32), ALU.subtract)
                        chain.link(dve.tensor_tensor(near[:, s, 1], near[:, s, 1], mround[:].bitcast(F32), ALU.subtract))
                    elif is_lsh:
                        chain.link(dve.tensor_copy(mround[:], smax[:, s]))
                    else:
                        chain.link(dve.tensor_tensor(mround[:], smax[:, s], pad_score[:], ALU.max))
                        chain.link(dve.tensor_tensor(near[:, s, 0], pad_score[:], mround[:].bitcast(F32), ALU.subtract))
                    if s or rel or not first(it, u):
                        dve.wait_ge(misc_done, misc_number(it, u, f"neg{s}"))
                    for t in range(2):
                        last = dve.tensor_scalar(mneg[:, t, :, 24:28],
                                                 mround[:, t, :].bitcast(F32).rearrange("p (a j) -> p j a", j=4),
                                                 -1.0, None, ALU.mult)
                    last.then_inc(m_made, 1)
                    dve.wait_ge(misc_done, misc_number(it, u, f"neg{s}") + 1)
                    queries = stacks[:, 0, :, s * SEQ:(s + 1) * SEQ]
                    dve.tensor_tensor(queries, queries.bitcast(F32),
                                      bank[:, MISC, 0:SEQ].unsqueeze(1).to_broadcast([P, 4, SEQ]),
                                      ALU.add).then_inc(misc_out, 1)

                def attended(it, u, s):
                    g = it * 2 + u
                    dve.wait_ge(o_turned, g * 2 + (s + 1))
                    if not is_lsh:
                        dve.wait_ge(near_exp, g * 2 + (s + 1))
                    heads = lambda ap: ap.rearrange("p t (h d) -> p t h d", h=H)
                    wide = lambda ap: ap.unsqueeze(3).to_broadcast([P, 2, H, DH])
                    tiles = slice(2 * s, 2 * s + 2)
                    if rel:
                        dve.tensor_tensor(den[:], o_view[:, :, :, DH], near_e[:, s, 0], ALU.add)
                        dve.tensor_tensor(heads(part[:, 0]), heads(v_near[:, 0, tiles]), wide(near_e[:, s, 0]), ALU.mult)
                        chain.link(dve.tensor_tensor(heads(part[:, 1]), heads(v_near[:, 1, tiles]), wide(near_e[:, s, 1]), ALU.mult))
                        dve.tensor_tensor(heads(part[:, 0]), heads(part[:, 0]), o_view[:, :, :, 0:DH], ALU.add)
                        chain.link(dve.tensor_tensor(den[:], den[:], near_e[:, s, 1], ALU.add))
                        dve.tensor_tensor(part[:, 0], part[:, 0], part[:, 1], ALU.add)
                        chain.link(dve.reciprocal(den[:], den[:]))
                        num = heads(part[:, 0])
                        dve.tensor_tensor(heads(att[:, s]), num, wide(den[:]), ALU.mult).then_inc(att_made, 1)
                    elif is_lsh:
                        chain.link(dve.reciprocal(den[:], o_view[:, :, :, DH]))
                        dve.tensor_tensor(heads(att[:, s]), o_view[:, :, :, 0:DH], wide(den[:]), ALU.mult).then_inc(att_made, 1)
                    else:
                        chain.link(dve.tensor_tensor(near_e[:, s, 0], near_e[:, s, 0], pad_count[:], ALU.mult))
                        chain.link(dve.tensor_tensor(den[:], near_e[:, s, 0], o_view[:, :, :, DH], ALU.add))
                        chain.link(dve.reciprocal(den[:], den[:]))
                        dve.tensor_tensor(heads(att[:, s]), o_view[:, :, :, 0:DH], wide(den[:]), ALU.mult).then_inc(att_made, 1)
                    dve.wait_ge(att_made, g * 2 + (s + 1))

                def residual(it, u):
                    g = it * 2 + u
                    dve.wait_ge(y_done, g + 1)
                    frame.wait_loaded(dve, it, u)
                    chain.link(dve.tensor_tensor(core.acc[:].rearrange("p t d -> p (t d)"), bank[:, O_BANK, :],
                                                 core.xr[:, u].rearrange("p t d -> p (t d)"), ALU.add))
                    frame.norm(nc, dve, chain, it, u)

                def body(it, u):
                    g = it * 2 + u
                    chain.begin(it, u)
                    if not first(it, u):
                        attended(*frame.previous(it, u), 1)
                    if is_lsh:
                        make_buckets(it, u)
                    else:
                        split(it, u)
                    if rel:
                        products(it, u)
                    for n in range(1, 8, 2):
                        dve.wait_ge(stack_done, g * 8 + n + 1)
                        width = slice(0, 2 * P) if is_lsh and n >= 4 else slice(0, GT)
                        if n < 4:
                            dve.tensor_copy(stacks[:, 0, n, width], bank[:, P_BANKS[1], width]).then_inc(stack_v, 1)
                        else:
                            dve.tensor_scalar(stacks[:, 1, n - 4, width], bank[:, P_BANKS[1], width],
                                              core.one_row[:, n - 4:n - 3], None, ALU.add).then_inc(stack_v, 1)
                    if not first(it, u):
                        residual(*frame.previous(it, u))
                    for pair in range(8):
                        maxima(it, u, 0, pair)
                    shifts(it, u, 0)
                    for pair in range(8):
                        maxima(it, u, 1, pair)
                    shifts(it, u, 1)
                    attended(it, u, 0)
                    chain.end()

                for_groups(dve, core.groups, body)
                last = (core.groups // 2 - 1, 1)
                chain.begin(core.groups // 2, 0)
                attended(*last, 1)
                residual(*last)


def ternary_ffn(core, name, w, out=None):
    nc, bank = core.nc, core.bank
    F = 4
    UP1, UP2, DEEP, DOWN, TURN = 0, 2, 4, 6, 7
    with ExitStack() as ctx:
        frame = Frame(core, ctx, name, out)
        sem = lambda n: core.sem(ctx, f"{name}_{n}")
        sb = lambda n, s, d=F32: core.sbuf(ctx, f"{name}_{n}", s, d)
        up_done, silu_done, hid_done = sem("up_done"), sem("silu_done"), sem("hid_done")
        deep_done, gelu_done, y_done = sem("deep_done"), sem("gelu_done"), sem("y_done")
        dve_chain, pre, pre_pe = sem("dve_chain"), sem("pre"), sem("pre_pe")
        silu = sb("silu", [P, 2, GT])
        hid = sb("hid", [P, F, GT])
        deep = sb("deep", [P, 2, F, GT])
        out_scale = sb("out_scale", [P, P])

        with nc.Block() as block:
            @block.sync
            def _(sp):
                for_groups(sp, core.groups, lambda it, u: frame.load(sp, it, u, up_done, 2 * F))

            @block.gpsimd
            def _(pool):
                frame.pool(pool)

            @block.tensor
            def _(pe):
                pe.wait_ge(core.ffn_in, core.wide_loads)
                pe.matmul(bank[:, TURN, 0:P], core.ones_row[:], w["f3_w3s"][:], start=True, stop=True).then_inc(pre_pe, 1)
                pe.wait_ge(pre, 1)

                def down(it, u):
                    g = it * 2 + u
                    pe.wait_ge(gelu_done, (g + 1) * 2 * F)
                    if not first(it, u):
                        pe.wait_ge(frame.norm_done, g)
                    for t in range(TILES):
                        for f in range(F):
                            last = pe.matmul(bank[:, DOWN, t * P:(t + 1) * P], deep[:, 1, f, t * P:(t + 1) * P],
                                             w["f3_w3"][:, f, :], start=(t == 0 and f == 0), stop=(f == F - 1),
                                             skip_group_check=True)
                    last.then_inc(y_done, 1)

                def body(it, u):
                    g = it * 2 + u
                    xg = core.xg[:, u, 8:]
                    frame.wait_loaded(pe, it, u)
                    for f in range(F):
                        if not (first(it, u) and f < 2):
                            pe.wait_ge(hid_done, g * F + (f - 1))
                        pe.matmul(bank[:, UP1 + f % 2, :], w["f3_w1"][:, f * P:(f + 1) * P], xg, start=True,
                                  stop=True).then_inc(up_done, 1)
                        pe.matmul(bank[:, UP2 + f % 2, :], w["f3_w2"][:, f * P:(f + 1) * P], xg, start=True,
                                  stop=True).then_inc(up_done, 1)
                    if not first(it, u):
                        down(*frame.previous(it, u))
                    for layer in range(2):
                        weights, x = (w["f3_h1"], hid) if layer == 0 else (w["f3_h2"], deep[:, 0])
                        if layer == 0:
                            pe.wait_ge(hid_done, (g + 1) * F)
                        else:
                            pe.wait_ge(gelu_done, g * 2 * F + F)
                        for o in range(F):
                            n = layer * F + o
                            if not (first(it, u) and n < 2):
                                pe.wait_ge(gelu_done, g * 2 * F + (n - 1))
                            for f in range(F):
                                last = pe.matmul(bank[:, DEEP + n % 2, :], weights[:, f, o * P:(o + 1) * P], x[:, f, :],
                                                 start=(f == 0), stop=(f == F - 1))
                            last.then_inc(deep_done, 1)
                        if layer == 0 and not first(it, u):
                            frame.turn(pe, TURN, *frame.previous(it, u))

                for_groups(pe, core.groups, body)
                down(core.groups // 2 - 1, 1)
                frame.turn(pe, TURN, core.groups // 2 - 1, 1)

            @block.scalar
            def _(act):
                def body(it, u):
                    g = it * 2 + u
                    for f in range(F):
                        act.wait_ge(up_done, g * 2 * F + 2 * f + 1)
                        if not (first(it, u) and f < 2):
                            act.wait_ge(hid_done, g * F + (f - 1))
                        act.activation(silu[:, f % 2, :], bank[:, UP1 + f % 2, :], ACT.Silu,
                                       scale=w["f3_w1s"][:, f:f + 1]).then_inc(silu_done, 1)
                    for n in range(2 * F):
                        if n == F and not first(it, u):
                            act.wait_ge(y_done, g)
                            frame.store(act, TURN, *frame.previous(it, u))
                        scales = w["f3_h1s"] if n < F else w["f3_h2s"]
                        act.wait_ge(deep_done, g * 2 * F + n + 1)
                        act.activation(deep[:, n // F, n % F, :], bank[:, DEEP + n % 2, :], ACT.Gelu,
                                       scale=scales[:, n % F:n % F + 1]).then_inc(gelu_done, 1)

                frame.begin(act)
                for_groups(act, core.groups, body)
                frame.store(act, TURN, core.groups // 2 - 1, 1)
                frame.finish(act)

            @block.vector
            def _(dve):
                chain = Chain(dve, dve_chain, 3, 3)
                dve.wait_ge(pre_pe, 1)
                dve.tensor_copy(out_scale[:], bank[:, TURN, 0:P]).then_inc(pre, 1)
                dve.wait_ge(pre, 1)

                def residual(it, u):
                    g = it * 2 + u
                    dve.wait_ge(y_done, g + 1)
                    frame.wait_loaded(dve, it, u)
                    chain.link(dve.tensor_tensor(core.acc[:], bank[:, DOWN, :].rearrange("p (t d) -> p t d", d=P),
                                                 out_scale[:].unsqueeze(1).to_broadcast([P, TILES, P]), ALU.mult))
                    chain.link(dve.tensor_tensor(core.acc[:], core.acc[:], core.xr[:, u], ALU.add))
                    frame.norm(nc, dve, chain, it, u)

                def body(it, u):
                    g = it * 2 + u
                    chain.begin(it, u)
                    for f in range(F):
                        dve.wait_ge(silu_done, g * F + f + 1)
                        dve.wait_ge(up_done, g * 2 * F + 2 * f + 2)
                        dve.scalar_tensor_tensor(out=hid[:, f, :], in0=bank[:, UP2 + f % 2, :],
                                                 scalar=w["f3_w2s"][:, f:f + 1], in1=silu[:, f % 2, :],
                                                 op0=ALU.mult, op1=ALU.mult).then_inc(hid_done, 1)
                    if not first(it, u):
                        residual(*frame.previous(it, u))
                    chain.end()

                for_groups(dve, core.groups, body)
                chain.begin(core.groups // 2, 0)
                residual(core.groups // 2 - 1, 1)


def butterfly_ffn(core, name, w, D, out=None):
    nc, bank = core.nc, core.bank
    F = 4
    WIDTH = F * P
    STAGES = 9
    UP, DOWN, TURN = 0, 2, 7
    with ExitStack() as ctx:
        frame = Frame(core, ctx, name, out)
        sem = lambda n: core.sem(ctx, f"{name}_{n}")
        sb = lambda n, s, d=F32: core.sbuf(ctx, f"{name}_{n}", s, d)
        up_done, gelu_done, y_done = sem("up_done"), sem("gelu_done"), sem("y_done")
        dve_chain, pre, pre_pe = sem("dve_chain"), sem("pre"), sem("pre_pe")
        w_in = [sem("w_in0"), sem("w_in1")]
        stage_done, row_done, pool_step = sem("stage_done"), sem("row_done"), sem("pool_step")
        wst = sb("wst", [P, 2, 2, 2 * WIDTH])
        both = sb("both", [P, 2, 2, WIDTH])
        tmp = sb("tmp", [P, 2, 2, 2, WIDTH // 2])
        row = sb("row", [1, 2, WIDTH])
        rtmp = sb("rtmp", [1, 4, WIDTH // 2])
        upb = sb("upb", [P, F])
        wdown = sb("wdown", [P, F, P])
        ybias = sb("ybias", [1, P])
        hid = sb("hid", [P, 2, F, GT])

        with nc.Block() as block:
            @block.sync
            def _(sp):
                for n in range(STAGES):
                    if n >= 2:
                        sp.wait_ge(w_in[n % 2], 32 * (n // 2))
                        sp.wait_ge(stage_done, n - 1)
                        sp.wait_ge(row_done, n - 1)
                    sp.dma_start(wst[:, n % 2, 0, :], D["f2_up"][n:n + 1, :].to_broadcast([P, 2 * WIDTH])).then_inc(w_in[n % 2], 16)
                    k = STAGES - 1 - n
                    sp.dma_start(wst[:, n % 2, 1, :], D["f2_down"][k:k + 1, :].to_broadcast([P, 2 * WIDTH])).then_inc(w_in[n % 2], 16)
                for_groups(sp, core.groups, lambda it, u: frame.load(sp, it, u, up_done, F))

            @block.gpsimd
            def _(pool):
                count = 0
                pool.tensor_copy(row[:, 0, :], w["f2_bexp"][:]).then_inc(pool_step, 1)
                count += 1
                for n in range(STAGES):
                    s = 2 ** n
                    pool.wait_ge(w_in[n % 2], 32 * (n // 2 + 1))
                    pool.wait_ge(pool_step, count)
                    y = row[:, n % 2].rearrange("p (b t s) -> p b t s", t=2, s=s)
                    o = row[:, (n + 1) % 2].rearrange("p (b t s) -> p b t s", t=2, s=s)
                    m = wst[0:1, n % 2, 0].rearrange("p (b s i j) -> p b s i j", s=s, i=2, j=2)
                    v = lambda k: rtmp[:, k].rearrange("p (b s) -> p b s", s=s)
                    for i in range(2):
                        for j in range(2):
                            last = pool.tensor_tensor(v(2 * i + j), m[:, :, :, i, j], y[:, :, j, :], ALU.mult)
                    last.then_inc(pool_step, 1)
                    count += 1
                    pool.wait_ge(pool_step, count)
                    for i in range(2):
                        last = pool.tensor_tensor(o[:, :, i, :], v(2 * i), v(2 * i + 1), ALU.add)
                    last.then_inc(row_done, 1)
                    pool.wait_ge(row_done, n + 1)
                pool.tensor_tensor(row[:, 0, :], row[:, STAGES % 2, :], w["f2_upb"][:], ALU.add)
                pool.tensor_tensor(ybias[:], w["f2_bcon"][:], w["f2_downb"][:], ALU.add).then_inc(row_done, 1)
                frame.pool(pool)

            @block.tensor
            def _(pe):
                pe.wait_ge(row_done, STAGES + 1)
                for f in range(F):
                    pe.matmul(bank[:, TURN, f:f + 1], row[0:1, 0, f * P:(f + 1) * P], core.ones_row[0:1, 0:1],
                              start=(f == 0), stop=True, skip_group_check=True)
                pe.wait_ge(stage_done, STAGES)
                for f in range(F):
                    last = pe.transpose(bank[:, UP, f * P:(f + 1) * P], both[:, STAGES % 2, 1, f * P:(f + 1) * P], core.ident[:])
                last.then_inc(pre_pe, 1)
                pe.wait_ge(pre, 1)

                def down(it, u):
                    g = it * 2 + u
                    pe.wait_ge(gelu_done, (g + 1) * F)
                    if not first(it, u):
                        pe.wait_ge(frame.norm_done, g)
                    for t in range(TILES):
                        for f in range(F):
                            pe.matmul(bank[:, DOWN, t * P:(t + 1) * P], hid[:, u, f, t * P:(t + 1) * P],
                                      wdown[:, f, :], start=(t == 0 and f == 0), stop=False, skip_group_check=True)
                        last = pe.matmul(bank[:, DOWN, t * P:(t + 1) * P], core.ones_row[:], ybias[:],
                                         start=False, stop=True, skip_group_check=True)
                    last.then_inc(y_done, 1)

                def body(it, u):
                    g = it * 2 + u
                    xg = core.xg[:, u, 8:]
                    frame.wait_loaded(pe, it, u)
                    for f in range(F):
                        if not (first(it, u) and f < 2):
                            pe.wait_ge(gelu_done, g * F + (f - 1))
                        pe.matmul(bank[:, UP + f % 2, :], both[:, STAGES % 2, 0, f * P:(f + 1) * P], xg, start=True,
                                  stop=True).then_inc(up_done, 1)
                    if not first(it, u):
                        frame.turn(pe, TURN, *frame.previous(it, u))
                    down(it, u)

                for_groups(pe, core.groups, body)
                frame.turn(pe, TURN, core.groups // 2 - 1, 1)

            @block.scalar
            def _(act):
                def body(it, u):
                    g = it * 2 + u
                    for f in range(F):
                        act.wait_ge(up_done, g * F + f + 1)
                        if not peeled(it):
                            act.wait_ge(y_done, g - 1)
                        act.activation(hid[:, u, f, :], bank[:, UP + f % 2, :], ACT.Gelu,
                                       bias=upb[:, f:f + 1]).then_inc(gelu_done, 1)
                    if not first(it, u):
                        frame.store(act, TURN, *frame.previous(it, u))

                frame.begin(act)
                act.wait_ge(pre, 1)
                for_groups(act, core.groups, body)
                frame.store(act, TURN, core.groups // 2 - 1, 1)
                frame.finish(act)

            @block.vector
            def _(dve):
                pre_chain = sem("pre_chain")
                step = Chain(dve, pre_chain, 0)
                dve.tensor_copy(both[:, 0, 0, :], w["f2_wexp"][:])
                step.link(dve.tensor_copy(both[:, 0, 1, :], w["f2_wcon"][:]))
                for n in range(STAGES):
                    dve.wait_ge(w_in[n % 2], 32 * (n // 2 + 1))
                    for side, s in enumerate((2 ** n, 2 ** (STAGES - 1 - n))):
                        y = both[:, n % 2, side].rearrange("p (b t s) -> p b t s", t=2, s=s)
                        m = wst[:, n % 2, side].rearrange("p (b s i j) -> p b s i j", s=s, i=2, j=2)
                        for i in range(2):
                            for j in range(2):
                                k = (i, j) if side == 0 else (j, i)
                                last = dve.tensor_tensor(tmp[:, side, i, j].rearrange("p (b s) -> p b s", s=s),
                                                         m[:, :, :, k[0], k[1]], y[:, :, j, :], ALU.mult)
                    step.link(last)
                    for side, s in enumerate((2 ** n, 2 ** (STAGES - 1 - n))):
                        o = both[:, (n + 1) % 2, side].rearrange("p (b t s) -> p b t s", t=2, s=s)
                        for i in range(2):
                            v = lambda j: tmp[:, side, i, j].rearrange("p (b s) -> p b s", s=s)
                            last = dve.tensor_tensor(o[:, :, i, :], v(0), v(1), ALU.add)
                    last.then_inc(stage_done, 1)
                    dve.wait_ge(stage_done, n + 1)
                dve.wait_ge(pre_pe, 1)
                dve.tensor_copy(upb[:], bank[:, TURN, 0:F])
                dve.tensor_copy(wdown[:].rearrange("p f d -> p (f d)"), bank[:, UP, :]).then_inc(pre, 1)

                chain = Chain(dve, dve_chain, 2)

                def body(it, u):
                    g = it * 2 + u
                    chain.begin(it, u)
                    dve.wait_ge(y_done, g + 1)
                    frame.wait_loaded(dve, it, u)
                    chain.link(dve.tensor_tensor(core.acc[:].rearrange("p t d -> p (t d)"), bank[:, DOWN, :],
                                                 core.xr[:, u].rearrange("p t d -> p (t d)"), ALU.add))
                    frame.norm(nc, dve, chain, it, u)
                    chain.end()

                for_groups(dve, core.groups, body)


def hilbert_attention(core, name, w, out=None):
    nc, bank = core.nc, core.bank
    BLOCK, SEG, DIL = 64, 32, 4
    NB = SEQ // BLOCK
    S = SEG // DIL
    SCALE = float(DH) ** -0.5
    XSEL, Q, SCORES, V, DEN, ATT = 0, 2, 3, 4, 6, 7
    with ExitStack() as ctx:
        frame = Frame(core, ctx, name, out)
        sem = lambda n: core.sem(ctx, f"{name}_{n}")
        sb = lambda n, s, d=F32: core.sbuf(ctx, f"{name}_{n}", s, d)
        sel_done = sem("sel_done")
        xk_out, xkr_out, xq_out = sem("xk_out"), sem("xkr_out"), sem("xq_out")
        q_done, q_out = sem("q_done"), sem("q_out")
        k_done, k_out, kbd_made = sem("k_done"), sem("k_out"), sem("kbd_made")
        v_done, v_made = sem("v_done"), sem("v_made")
        s_done, sc_read = sem("s_done"), sem("sc_read")
        sub_made, exp_done = sem("sub_made"), sem("exp_done")
        att_done, att_out, y_done = sem("att_done"), sem("att_out"), sem("y_done")
        dve_chain, pre, pre_pe, counted = sem("dve_chain"), sem("pre"), sem("pre_pe"), sem("counted")
        mapc = sb("mapc", [P, 2])
        mapr = sb("mapr", [1, SEQ])
        map_cols = sb("map_cols", [P, 2, P])
        pos = sb("pos", [P, 2])
        offs = sb("offs", [P, NB, S])
        thr = sb("thr", [P, SEQ // SEG + 1])
        over = sb("over", [P, NB, SEQ // SEG + 1])
        seg = sb("seg", [P, NB])
        inside = sb("inside", [P, NB])
        kp = sb("kp", [P, NB, S])
        at = sb("at", [P, 2, NB * S])
        idx = sb("idx", [P, SEQ + NB * S])
        wrap = sb("wrap", [P, SEQ + NB * S])
        sel = sb("sel", [P, 2, SEQ + NB * S])
        khead = sb("khead", [P, NB, H])
        vhead = sb("vhead", [P, NB, P])
        vbias = sb("vbias", [P, NB, P])
        vhead_all = sb("vhead_all", [P, H, DH])
        valid = sb("valid", [P, SEQ])
        invalid = sb("invalid", [P, SEQ])
        bqs = sb("bqs", [P, 1])
        xq = sb("xq", [P, GT])
        xk = sb("xk", [P, 2 * NB * S])
        xkr = sb("xkr", [P, 2 * NB, H, S])
        qt = sb("qt", [P, GT])
        kx = sb("kx", [P, 2 * NB, S])
        kbd = sb("kbd", [P, 2 * NB, H, S])
        vbd = sb("vbd", [P, 2, 2 * NB, P])
        prob = sb("prob", [P, 2 * NB, BLOCK])
        smax = sb("smax", [P, 2 * NB])
        den = sb("den", [P, GT])
        attt = sb("attt", [P, GT])

        with nc.Block() as block:
            @block.sync
            def _(sp):
                for_groups(sp, core.groups, lambda it, u: frame.load(sp, it, u, sel_done, 2))

            @block.gpsimd
            def _(pool):
                pool.iota(pos[:], pattern=[[P, 2]], base=0, channel_multiplier=1, allow_small_or_imprecise_dtypes=True)
                pool.iota(offs[:], pattern=[[0, NB], [DIL, S]], base=0, channel_multiplier=0,
                          allow_small_or_imprecise_dtypes=True)
                pool.iota(thr[:], pattern=[[SEG, SEQ // SEG + 1]], base=0, channel_multiplier=0,
                          allow_small_or_imprecise_dtypes=True).then_inc(counted, 1)
                frame.pool(pool)

            @block.tensor
            def _(pe):
                pe.wait_ge(pre, 1)
                pe.matmul(bank[:, 0, 0:SEQ], core.ones_row[:], mapr[:], start=True, stop=True)
                pe.matmul(bank[:, 1, 0:P], core.ones_row[:], w["l2_bv"][:], start=True, stop=True).then_inc(pre_pe, 1)
                pe.wait_ge(pre, 2)
                for t in range(2):
                    last = pe.matmul(bank[:, 2, 0:NB * S], map_cols[:, t, :], at[:, t, :], start=(t == 0), stop=(t == 1))
                last.then_inc(pre_pe, 1)
                pe.wait_ge(pre, 3)

                def select(it, u):
                    frame.wait_loaded(pe, it, u)
                    for s in range(2):
                        for t in range(2):
                            last = pe.matmul(bank[:, XSEL + s, 0:SEQ + NB * S], core.xr[:, u, 2 * s + t, :], sel[:, t, :],
                                             start=(t == 0), stop=(t == 1))
                        last.then_inc(sel_done, 1)

                def project(it, u):
                    g = it * 2 + u
                    pe.wait_ge(xk_out, 2 * g + 2)
                    if not first(it, u):
                        pe.wait_ge(sc_read, g)
                    pe.matmul(bank[:, SCORES, 0:2 * NB * S], w["l2_wqkv"][:, P:2 * P], xk[:], start=True,
                              stop=True).then_inc(k_done, 1)
                    pe.wait_ge(xq_out, 2 * g + 2)
                    if not peeled(it) and out is None:
                        pe.wait_ge(frame.turned_out, g - 1)
                    pe.matmul(bank[:, Q, :], w["l2_wqkv"][:, 0:P], xq[:], start=True, stop=True).then_inc(q_done, 1)
                    pe.wait_ge(xkr_out, 2 * g + 2)
                    if not first(it, u):
                        pe.wait_ge(v_made, g)
                    for s in range(2):
                        for b in range(NB):
                            last = pe.matmul(bank[:, V + s, b * P:(b + 1) * P],
                                             xkr[:, s * NB + b].rearrange("p h s -> p (h s)"), w["l2_wqkv"][:, 2 * P:3 * P],
                                             start=(b == 0), stop=True, skip_group_check=True)
                        last.then_inc(v_done, 1)

                def weigh(it, u):
                    g = it * 2 + u
                    pe.wait_ge(exp_done, g + 1)
                    pe.wait_ge(v_made, g + 1)
                    if not first(it, u):
                        pe.wait_ge(frame.norm_done, g)
                    pe.matmul(bank[:, DEN, :], vhead_all[:].rearrange("p h d -> p (h d)"), prob[:].rearrange("p b m -> p (b m)"),
                              start=True, stop=True)
                    for b in range(2 * NB):
                        last = pe.matmul(bank[:, ATT, b * BLOCK:(b + 1) * BLOCK], vbd[:, u, b, :], prob[:, b, :],
                                         start=(b == 0), stop=True, skip_group_check=True)
                    last.then_inc(att_done, 1)

                def scores(it, u):
                    g = it * 2 + u
                    pe.wait_ge(q_out, g + 1)
                    pe.wait_ge(kbd_made, g + 1)
                    for b in range(2 * NB):
                        last = pe.matmul(bank[:, SCORES, b * BLOCK:(b + 1) * BLOCK], kbd[:, b].rearrange("p h s -> p (h s)"),
                                         qt[:, b * BLOCK:(b + 1) * BLOCK], start=(b == 0), stop=True,
                                         skip_group_check=True)
                    last.then_inc(s_done, 1)

                def output(it, u):
                    g = it * 2 + u
                    pe.wait_ge(att_out, g + 1)
                    for t in range(TILES):
                        pe.matmul(bank[:, DEN, t * P:(t + 1) * P], attt[:, t * P:(t + 1) * P], w["l2_wo"][:],
                                  start=(t == 0), stop=False, skip_group_check=True)
                        last = pe.matmul(bank[:, DEN, t * P:(t + 1) * P], core.ones_row[:], w["l2_bo"][:],
                                         start=False, stop=True, skip_group_check=True)
                    last.then_inc(y_done, 1)

                def body(it, u):
                    select(it, u)
                    if not first(it, u):
                        weigh(*frame.previous(it, u))
                    project(it, u)
                    scores(it, u)
                    if not first(it, u):
                        output(*frame.previous(it, u))
                        frame.turn(pe, Q, *frame.previous(it, u))

                for_groups(pe, core.groups, body)
                last = (core.groups // 2 - 1, 1)
                weigh(*last)
                output(*last)
                frame.turn(pe, Q, *last)

            @block.scalar
            def _(act):
                def body(it, u):
                    g = it * 2 + u
                    if not first(it, u):
                        act.wait_ge(k_done, g)
                        act.wait_ge(q_done, g)
                        act.wait_ge(v_done, 2 * g)
                    for s in range(2):
                        act.wait_ge(sel_done, 2 * g + s + 1)
                        keys = bank[:, XSEL + s, SEQ:SEQ + NB * S]
                        act.copy(xk[:, s * NB * S:(s + 1) * NB * S], keys).then_inc(xk_out, 1)
                    for s in range(2):
                        act.copy(xq[:, s * SEQ:(s + 1) * SEQ], bank[:, XSEL + s, 0:SEQ]).then_inc(xq_out, 1)
                    for s in range(2):
                        keys = bank[:, XSEL + s, SEQ:SEQ + NB * S].rearrange("p (b s) -> p b s", s=S)
                        act.copy(xkr[:, s * NB:(s + 1) * NB], keys.unsqueeze(2).to_broadcast([P, NB, H, S])).then_inc(xkr_out, 1)
                    act.wait_ge(k_done, g + 1)
                    if not first(it, u):
                        act.wait_ge(kbd_made, g)
                    act.activation(kx[:].rearrange("p b s -> p (b s)"), bank[:, SCORES, 0:2 * NB * S], ACT.Identity,
                                   bias=w["l2_bqk"][:, 1:2]).then_inc(k_out, 1)
                    act.wait_ge(q_done, g + 1)
                    if not first(it, u):
                        act.wait_ge(s_done, g)
                    act.activation(qt[:], bank[:, Q, :], ACT.Identity, bias=bqs[:], scale=SCALE).then_inc(q_out, 1)
                    act.wait_ge(sub_made, g + 1)
                    act.activation(prob[:], prob[:], ACT.Exp).then_inc(exp_done, 1)
                    if not first(it, u):
                        frame.store(act, Q, *frame.previous(it, u))

                frame.begin(act)
                act.wait_ge(pre, 3)
                for_groups(act, core.groups, body)
                last = (core.groups // 2 - 1, 1)
                frame.store(act, Q, *last)
                frame.finish(act)

            @block.vector
            def _(dve):
                pre_chain = sem("pre_chain")
                step = Chain(dve, pre_chain, 0)
                dve.tensor_copy(mapr[:], w["l2_mapr"][:])
                step.link(dve.tensor_copy(mapc[:], w["l2_mapc"][:]))
                dve.tensor_scalar(mapr[:], mapr[:], -512.0, 512.0, ALU.max, ALU.min)
                step.link(dve.tensor_scalar(mapc[:], mapc[:], -512.0, 512.0, ALU.max, ALU.min))
                dve.tensor_scalar(bqs[:], w["l2_bqk"][:, 0:1], SCALE, None, ALU.mult)
                dve.tensor_copy(map_cols[:], mapc[:].unsqueeze(2).to_broadcast([P, 2, P])).then_inc(pre, 1)
                dve.wait_ge(pre, 1)
                dve.wait_ge(pre_pe, 1)
                dve.wait_ge(counted, 1)
                step.link(dve.tensor_copy(idx[:, 0:SEQ], bank[:, 0, 0:SEQ]))
                dve.tensor_scalar(valid[:], idx[:, 0:SEQ], float(SEQ), None, ALU.is_lt)
                lead = idx[:, 0:SEQ].rearrange("p (b m) -> p b m", m=BLOCK)[:, :, 0]
                NT = SEQ // SEG + 1
                step.link(dve.tensor_tensor(over[:], lead.unsqueeze(2).to_broadcast([P, NB, NT]),
                                            thr[:].unsqueeze(1).to_broadcast([P, NB, NT]), ALU.is_ge))
                step.link(dve.tensor_reduce(seg[:], over[:], AX_X, ALU.add))
                dve.tensor_scalar(invalid[:], valid[:], -1.0, -NEG, ALU.add, ALU.mult)
                dve.tensor_copy(vhead_all[:], core.head_of[:].unsqueeze(2).to_broadcast([P, H, DH]))
                dve.tensor_scalar(inside[:], lead, float(SEQ), None, ALU.is_lt)
                step.link(dve.tensor_scalar(seg[:], seg[:], float(SEG), -float(SEG), ALU.mult, ALU.add))
                step.link(dve.tensor_tensor(kp[:], offs[:], seg[:].unsqueeze(2).to_broadcast([P, NB, S]), ALU.add))
                step.link(dve.tensor_scalar(kp[:], kp[:], 0.0, float(SEQ - 1), ALU.max, ALU.min))
                for t in range(2):
                    last = dve.tensor_scalar(at[:, t, :], kp[:].rearrange("p b s -> p (b s)"), pos[:, t:t + 1], None, ALU.is_equal)
                last.then_inc(pre, 1)
                dve.tensor_tensor(khead[:], core.head_of[:].unsqueeze(1).to_broadcast([P, NB, H]),
                                  inside[:].unsqueeze(2).to_broadcast([P, NB, H]), ALU.mult)
                dve.wait_ge(pre_pe, 2)
                step.link(dve.tensor_copy(idx[:, SEQ:], bank[:, 2, 0:NB * S]))
                step.link(dve.tensor_scalar(wrap[:], idx[:], 0.0, float(SEQ), ALU.is_lt, ALU.mult))
                step.link(dve.tensor_tensor(idx[:], idx[:], wrap[:], ALU.add))
                step.link(dve.tensor_scalar(idx[:], idx[:], 0.0, float(SEQ - 1), ALU.max, ALU.min))
                for t in range(2):
                    dve.tensor_scalar(sel[:, t, :], idx[:], pos[:, t:t + 1], None, ALU.is_equal)
                step.link(dve.tensor_copy(vhead[:].rearrange("p b (h d) -> p b h d", h=H),
                                          khead[:].unsqueeze(3).to_broadcast([P, NB, H, DH])))
                dve.tensor_tensor(vbias[:], vhead[:], bank[:, 1, 0:P].unsqueeze(1).to_broadcast([P, NB, P]),
                                  ALU.mult).then_inc(pre, 1)
                dve.wait_ge(pre, 3)

                chain = Chain(dve, dve_chain, 7, 4)

                def attended(it, u):
                    g = it * 2 + u
                    dve.wait_ge(att_done, g + 1)
                    chain.link(dve.tensor_scalar(den[:], bank[:, DEN, :], 1e-6, None, ALU.add))
                    chain.link(dve.reciprocal(den[:], den[:]))
                    if not first(it, u):
                        dve.wait_ge(y_done, g)
                    dve.tensor_tensor(attt[:], bank[:, ATT, :], den[:], ALU.mult).then_inc(att_out, 1)

                def residual(it, u):
                    g = it * 2 + u
                    dve.wait_ge(y_done, g + 1)
                    frame.wait_loaded(dve, it, u)
                    chain.link(dve.tensor_tensor(core.acc[:].rearrange("p t d -> p (t d)"), bank[:, DEN, :],
                                                 core.xr[:, u].rearrange("p t d -> p (t d)"), ALU.add))
                    frame.norm(nc, dve, chain, it, u)

                def body(it, u):
                    g = it * 2 + u
                    chain.begin(it, u)
                    if not first(it, u):
                        attended(*frame.previous(it, u))
                    dve.wait_ge(k_out, g + 1)
                    if not first(it, u):
                        dve.wait_ge(s_done, g)
                    for s in range(2):
                        last = dve.tensor_tensor(kbd[:, s * NB:(s + 1) * NB],
                                                 kx[:, s * NB:(s + 1) * NB, :].unsqueeze(2).to_broadcast([P, NB, H, S]),
                                                 khead[:].unsqueeze(3).to_broadcast([P, NB, H, S]), ALU.mult)
                    last.then_inc(kbd_made, 1)
                    if not peeled(it):
                        dve.wait_ge(att_done, g - 1)
                    for s in range(2):
                        dve.wait_ge(v_done, 2 * g + s + 1)
                        last = dve.tensor_tensor(vbd[:, u, s * NB:(s + 1) * NB, :], bank[:, V + s, :].rearrange("p (b d) -> p b d", d=P),
                                                 vhead[:], ALU.mult)
                    chain.link(last)
                    for s in range(2):
                        last = dve.tensor_tensor(vbd[:, u, s * NB:(s + 1) * NB, :], vbd[:, u, s * NB:(s + 1) * NB, :], vbias[:], ALU.add)
                    last.then_inc(v_made, 1)
                    dve.wait_ge(s_done, g + 1)
                    blocks = bank[:, SCORES, :].rearrange("p (s m) -> p s m", m=SEQ)
                    both = prob[:].rearrange("p (s b) m -> p s (b m)", s=2)
                    twice = lambda ap: ap.unsqueeze(1).to_broadcast([P, 2, SEQ])
                    dve.tensor_tensor(both, blocks, twice(valid[:]), ALU.mult).then_inc(sc_read, 1)
                    dve.wait_ge(sc_read, g + 1)
                    chain.link(dve.tensor_tensor(both, both, twice(invalid[:]), ALU.add))
                    chain.link(dve.tensor_reduce(smax[:], prob[:], AX_X, ALU.max))
                    dve.tensor_tensor(prob[:], prob[:], smax[:].unsqueeze(2).to_broadcast([P, 2 * NB, BLOCK]),
                                      ALU.subtract).then_inc(sub_made, 1)
                    if not first(it, u):
                        residual(*frame.previous(it, u))
                    chain.end()

                for_groups(dve, core.groups, body)
                chain.begin(core.groups // 2, 0)
                attended(core.groups // 2 - 1, 1)
                residual(core.groups // 2 - 1, 1)


def _layout_rest(np, i):
    a = {}
    w, b = i["L2_attn_Wqkv"], i["L2_attn_bqkv"].reshape(3, P)
    a["l2_wqkv"] = w
    a["l2_bqk"] = b.T
    a["l2_bv"] = b[2:3]
    a["l2_wo"] = i["L2_attn_Wproj"]
    a["l2_bo"] = i["L2_attn_bproj"].reshape(1, P)
    a["l2_mapc"] = i["L2_attn_mapping"][:SEQ].reshape(2, P).T
    a["l2_mapr"] = i["L2_attn_mapping"][:SEQ].reshape(1, SEQ)
    a["f2_wexp"] = i["L2_ffn_W_exp"]
    a["f2_bexp"] = i["L2_ffn_b_exp"].reshape(1, -1)
    a["f2_up"] = i["L2_ffn_up_weights"].reshape(9, -1)
    a["f2_upb"] = i["L2_ffn_up_bias"].reshape(1, -1)
    a["f2_down"] = i["L2_ffn_down_weights"].reshape(9, -1)
    a["f2_wcon"] = i["L2_ffn_W_con"].T
    a["f2_bcon"] = i["L2_ffn_b_con"].reshape(1, P)
    a["f2_downb"] = i["L2_ffn_down_bias"].reshape(1, P)
    a["l3_wq"] = i["L3_attn_Wq"].T
    a["l3_wk"] = i["L3_attn_Wk"]
    kv = [i[n].T.reshape(P, H, DH) for n in ("L3_attn_Wk", "L3_attn_Wv")]
    a["l3_wkv"] = np.stack(kv, axis=2).reshape(P, -1)
    a["l3_wo"] = i["L3_attn_Wo"].T
    a["l3_bo"] = i["L3_attn_bo"].reshape(1, P)
    a["l3_planes"] = np.tile(i["L3_attn_planes_T"], (H, 1))
    a["l3_protos"] = np.tile(i["L3_attn_protos_T"], (32, 1))
    a["l3_temp"] = np.tile(i["L3_attn_logit_temp"].reshape(1, 1), (P, 1))
    for n in ("w1", "w2"):
        a["f3_" + n] = i[f"L3_ffn_{n}_w"].T
        a[f"f3_{n}s"] = i[f"L3_ffn_{n}_s"].reshape(-1, P).T
    for n in ("h1", "h2"):
        a["f3_" + n] = i[f"L3_ffn_{n}_w"].T.reshape(-1, P, 4 * P).transpose(1, 0, 2)
        a[f"f3_{n}s"] = i[f"L3_ffn_{n}_s"].reshape(-1, P).T
    a["f3_w3"] = i["L3_ffn_w3_w"].T.reshape(-1, P, P).transpose(1, 0, 2)
    a["f3_w3s"] = i["L3_ffn_w3_s"].reshape(1, P)
    return a


WIDE = {1: ("m0_w1", "m0_w3", "m0_w2"), 3: ("m1_w1", "m1_w3", "m1_w2"),
        7: ("f3_w1", "f3_w2", "f3_h1", "f3_h2", "f3_w3")}
PHASES = (0, 1, 2, 3, 4, 5, 6, 7)


def build(nc, D, out, phases=PHASES):
    with ExitStack() as ctx:
        groups = D["x"].shape[0] // GT
        core = Core(nc, ctx, groups)
        core.params_in = core.sem(ctx, "params_in")
        core.ffn_in = core.sem(ctx, "ffn_in")
        params = []
        w = {}
        for name in D:
            if name not in ("x", "f2_up", "f2_down") and name not in sum(WIDE.values(), ()):
                w[name] = core.sbuf(ctx, "w_" + name, list(D[name].shape), D[name].dtype)
                params.append((w[name][:], name))
        size = lambda n: int(D[n].shape[-1]) * (int(D[n].shape[1]) if len(D[n].shape) == 3 else 1)
        wide = core.sbuf(ctx, "wide", [P, max(sum(size(n) for n in names) for names in WIDE.values())])
        wide_loads = 0
        setup(core, D, params)
        attention_constants(core, D)
        core.end_phase()

        def load_wide(phase):
            at = 0
            with nc.Block() as block:
                @block.sync
                def _(sp):
                    nonlocal at
                    for name in WIDE[phase]:
                        view = wide[:, at:at + size(name)]
                        if len(D[name].shape) == 3:
                            view = view.rearrange("p (a b) -> p a b", b=int(D[name].shape[2]))
                        sp.dma_start(view, D[name]).then_inc(core.ffn_in, 16)
                        w[name] = view
                        at += size(name)

        result = out.rearrange("(t p) d -> p t d", p=P)
        loaded = []
        pending = [n for n in phases if n in WIDE]
        for n in phases:
            if pending and (len(pending) == len([p for p in phases if p in WIDE]) or n not in WIDE):
                if pending[0] not in loaded:
                    load_wide(pending[0])
                    loaded.append(pending[0])
                    wide_loads += len(WIDE[pending[0]])
            if n in WIDE:
                core.wide_loads = 16 * wide_loads
                pending.pop(0)
            last = result if n == phases[-1] else None
            if n == 0:
                attention(core, "a0", "rel", w["l0_wq"], w["l0_wk"], w["l0_wv"], w["l0_wo"], w["l0_bq"],
                          w["l0_bk"], w["l0_bv"], w["l0_bo"], w["l0_relk"], w["l0_relv"])
            if n == 2:
                q, b = w["l1_wqkv"], w["l1_bqk"]
                attention(core, "a1", "band", q[:, 0:P], q[:, P:2 * P], q[:, 2 * P:3 * P], w["l1_wo"],
                          b[:, 0:1], b[:, 1:2], w["l1_bv"], w["l1_bo"])
            if n == 1:
                moe(core, "m0", w["m0_w1"], w["m0_w3"], w["m0_w2"], w["m0_r"], w["m0_rb"], 4, last)
            if n == 6:
                attention(core, "a3", "lsh", w["l3_wq"], w["l3_wk"], w["l3_wkv"], w["l3_wo"], None, None, None,
                          w["l3_bo"], lsh=(w["l3_planes"], w["l3_protos"], w["l3_temp"]), out=last)
            if n == 7:
                ternary_ffn(core, "f3", w, last)
            if n == 5:
                butterfly_ffn(core, "f2", w, D, last)
            if n == 4:
                hilbert_attention(core, "a2", w, last)
            if n == 3:
                moe(core, "m1", w["m1_w1"], w["m1_w3"], w["m1_w2"], w["m1_r"], None, 8, last)
            if n != phases[-1]:
                core.end_phase()


def _layout(np, i):
    a = {}
    a["x"] = i["L0_attn_x"].reshape(-1, P)
    for n in "qkvo":
        a["l0_w" + n] = i["L0_attn_W_" + n]
    a["l0_bq"] = i["L0_attn_b_q"].reshape(P, 1)
    a["l0_bk"] = i["L0_attn_b_k"].reshape(P, 1)
    a["l0_bv"] = i["L0_attn_b_v"].reshape(1, P)
    a["l0_bo"] = i["L0_attn_b_o"].reshape(1, P)
    a["l0_relk"] = np.tile(i["L0_attn_rel_k_table"].T, (H, 1))
    a["l0_relv"] = np.tile(i["L0_attn_rel_v_table"], (1, H)).reshape(1, -1)
    a["m0_w1"] = i["L0_ffn_w1"].transpose(1, 0, 2).reshape(P, -1)
    a["m0_w3"] = i["L0_ffn_w3"].transpose(1, 0, 2).reshape(P, -1)
    a["m0_w2"] = i["L0_ffn_w2"].reshape(-1, P, P).transpose(1, 0, 2)
    a["m0_r"] = i["L0_ffn_router_w"]
    a["m0_rb"] = i["L0_ffn_router_b"].reshape(1, -1)
    a["l1_wqkv"] = i["L1_attn_Wqkv"].T
    a["l1_bqk"] = i["L1_attn_bqkv"].reshape(3, P).T
    a["l1_bv"] = i["L1_attn_bqkv"][2 * P:].reshape(1, P)
    a["l1_wo"] = i["L1_attn_Wout"].T
    a["l1_bo"] = i["L1_attn_bout"].reshape(1, P)
    h = i["L1_ffn_w3"].shape[-1]
    a["m1_w1"] = i["L1_ffn_w12"][:, :h].transpose(2, 0, 1).reshape(P, -1)
    a["m1_w3"] = i["L1_ffn_w12"][:, h:].transpose(2, 0, 1).reshape(P, -1)
    a["m1_w2"] = i["L1_ffn_w3"].transpose(0, 2, 1).reshape(-1, P, P).transpose(1, 0, 2)
    a["m1_r"] = i["L1_ffn_gate_w"].T
    a.update(_layout_rest(np, i))
    return {k: np.ascontiguousarray(v) for k, v in a.items()}


def kernel(**inputs):
    import numpy as np
    import concourse.bacc as bacc
    from concourse.bass_utils import run_bass_kernel_spmd

    nc = bacc.Bacc("TRN2", target_bir_lowering=False, num_devices=1)
    arrays = _layout(np, {k: np.asarray(v) for k, v in inputs.items()})
    D = {k: nc.dram_tensor("in_" + k, v.shape, mybir.dt.from_np(v.dtype), kind="ExternalInput").ap()
         for k, v in arrays.items()}
    shape = inputs["L0_attn_x"].shape
    out = nc.dram_tensor("out", arrays["x"].shape, F32, kind="ExternalOutput").ap()
    build(nc, D, out)
    r = run_bass_kernel_spmd(nc, [{"in_" + k: v for k, v in arrays.items()}], core_ids=[0])
    return r.results[0]["out"].reshape(shape)
```
